# Optimizing a Trainium2 kernel written in Bass

```python
import numpy as np
import jax
import jax.numpy as jnp

def _softmax(x, axis=-1):
    return jax.nn.softmax(x, axis=axis)

def _gelu(x):
    return jax.nn.gelu(x, approximate=True)

def _silu(x):
    return jax.nn.silu(x)

def _sigmoid(x):
    return jax.nn.sigmoid(x)

def _layernorm(x, axis=-1, eps=1e-05):
    m = jnp.mean(x, axis=axis, keepdims=True)
    v = jnp.var(x, axis=axis, keepdims=True)
    return (x - m) / jnp.sqrt(v + eps)

def _scatter_add(tgt, idx, src, axis=0):
    return tgt.at[idx].add(src)

def _segment_sum(src, seg, n):
    return jax.ops.segment_sum(src, seg, n)
kernel_name = 'mk_early_fusion_d1_tok_img1024_r4_230333'

def setup_inputs(seed: int=0):
    np.random.seed(seed)
    _w = jnp.asarray

    def _rec_inputs():
        import jax
        import jax.numpy as jnp
        _rk = jax.random.key(seed)
        x = -0.00016672 + 0.999947 * jax.random.normal(jax.random.fold_in(_rk, 1), (64, 3, 96, 96), jnp.float32)
        txt = 0.00180885 + 1.15405 * jax.random.normal(jax.random.fold_in(_rk, 2), (64, 32, 256), jnp.float32)
        return (x, txt)
    x, txt = _rec_inputs()

    def _L0_tok_setup():
        import jax, jax.numpy as jnp
        import numpy as np
        B, C, H, W = (64, 3, 96, 96)
        P = 16
        HP, WP = (H // P, W // P)
        N = HP * WP
        F = C * P * P
        D = 256
        key = jax.random.key(seed)
        k1, k2, k3, k4, k5 = jax.random.split(key, 5)
        data = jax.random.normal(k1, (B, C, H, W), dtype=jnp.float32)
        lim = 1.0 / np.sqrt(F)
        W_lin = jax.random.uniform(k2, (D, F), minval=-lim, maxval=lim, dtype=jnp.float32)
        b_lin = jax.random.uniform(k3, (D,), minval=-lim, maxval=lim, dtype=jnp.float32)
        class_token = jax.random.normal(k4, (1, 1, D), dtype=jnp.float32)
        position_embeddings = jax.random.normal(k5, (1, N + 1, D), dtype=jnp.float32)
        return {'data': data, 'W_lin': W_lin, 'b_lin': b_lin, 'class_token': class_token, 'position_embeddings': position_embeddings}
    _L0_tok_all = _L0_tok_setup()
    _L0_tok_in = {k: v for k, v in _L0_tok_all.items() if k in ('W_lin', 'b_lin', 'class_token', 'position_embeddings')}
    del _L0_tok_all

    def _L0_attn_setup():
        import jax, jax.numpy as jnp
        import numpy as np
        import math
        D_MODEL = 256
        N_HEADS = 16
        Q_PROJ = D_MODEL // 4
        KV_PROJ = D_MODEL // 4
        DH = D_MODEL // N_HEADS
        LN_EPS = 1e-05

        def _layernorm(x, gamma, beta):
            mu = jnp.mean(x, axis=-1, keepdims=True)
            var = jnp.mean(jnp.square(x - mu), axis=-1, keepdims=True)
            return (x - mu) * jax.lax.rsqrt(var + LN_EPS) * gamma + beta
        key = jax.random.key(seed)
        ks = jax.random.split(key, 7)
        B, S = (2, 512)
        x = jax.random.normal(ks[0], (B, S, D_MODEL), dtype=jnp.float32)
        W_dq = 0.01 * jax.random.normal(ks[1], (D_MODEL, Q_PROJ), dtype=jnp.float32)
        W_uq = 0.01 * jax.random.normal(ks[2], (Q_PROJ, D_MODEL), dtype=jnp.float32)
        W_dkv = 0.01 * jax.random.normal(ks[3], (D_MODEL, KV_PROJ), dtype=jnp.float32)
        W_ukv = 0.01 * jax.random.normal(ks[4], (KV_PROJ, 2 * D_MODEL), dtype=jnp.float32)
        W_o = 0.01 * jax.random.normal(ks[5], (D_MODEL, D_MODEL), dtype=jnp.float32)
        return {'x': x, 'W_dq': W_dq, 'W_uq': W_uq, 'q_ln_g': jnp.ones((Q_PROJ,), jnp.float32), 'q_ln_b': jnp.zeros((Q_PROJ,), jnp.float32), 'W_dkv': W_dkv, 'W_ukv': W_ukv, 'kv_ln_g': jnp.ones((KV_PROJ,), jnp.float32), 'kv_ln_b': jnp.zeros((KV_PROJ,), jnp.float32), 'W_o': W_o}
    _L0_attn_all = _L0_attn_setup()
    _L0_attn_in = {k: v for k, v in _L0_attn_all.items() if k in ('W_dq', 'W_uq', 'q_ln_g', 'q_ln_b', 'W_dkv', 'W_ukv', 'kv_ln_g', 'kv_ln_b', 'W_o')}
    del _L0_attn_all

    def _L0_ffn_setup():
        import jax, jax.numpy as jnp
        import numpy as np
        TOP_K = 2
        key = jax.random.key(seed)
        k1, k2, k3, k4 = jax.random.split(key, 4)
        B, T, D, H, E = (2, 512, 256, 512, 8)
        x = jax.random.normal(k1, (B, T, D), dtype=jnp.float32)
        w12 = jax.random.normal(k2, (E, 2 * H, D), dtype=jnp.float32) * D ** (-0.5)
        w3 = jax.random.normal(k3, (E, D, H), dtype=jnp.float32) * H ** (-0.5)
        gate_w = jax.random.normal(k4, (E, D), dtype=jnp.float32) * D ** (-0.5)
        return {'x': x, 'w12': w12, 'w3': w3, 'gate_w': gate_w}
    _L0_ffn_all = _L0_ffn_setup()
    _L0_ffn_in = {k: v for k, v in _L0_ffn_all.items() if k in ('w12', 'w3', 'gate_w')}
    del _L0_ffn_all
    return {'x': x, 'txt': txt, 'L0_tok_W_lin': _L0_tok_in['W_lin'], 'L0_tok_b_lin': _L0_tok_in['b_lin'], 'L0_tok_class_token': _L0_tok_in['class_token'], 'L0_tok_position_embeddings': _L0_tok_in['position_embeddings'], 'L0_attn_W_dq': _L0_attn_in['W_dq'], 'L0_attn_W_uq': _L0_attn_in['W_uq'], 'L0_attn_q_ln_g': _L0_attn_in['q_ln_g'], 'L0_attn_q_ln_b': _L0_attn_in['q_ln_b'], 'L0_attn_W_dkv': _L0_attn_in['W_dkv'], 'L0_attn_W_ukv': _L0_attn_in['W_ukv'], 'L0_attn_kv_ln_g': _L0_attn_in['kv_ln_g'], 'L0_attn_kv_ln_b': _L0_attn_in['kv_ln_b'], 'L0_attn_W_o': _L0_attn_in['W_o'], 'L0_ffn_w12': _L0_ffn_in['w12'], 'L0_ffn_w3': _L0_ffn_in['w3'], 'L0_ffn_gate_w': _L0_ffn_in['gate_w']}

def reference(x, txt, L0_tok_W_lin, L0_tok_b_lin, L0_tok_class_token, L0_tok_position_embeddings, L0_attn_W_dq, L0_attn_W_uq, L0_attn_q_ln_g, L0_attn_q_ln_b, L0_attn_W_dkv, L0_attn_W_ukv, L0_attn_kv_ln_g, L0_attn_kv_ln_b, L0_attn_W_o, L0_ffn_w12, L0_ffn_w3, L0_ffn_gate_w):
    import jax
    import jax.numpy as jnp

    def _L0_tok_ref(data, W_lin, b_lin, class_token, position_embeddings):
        import jax, jax.numpy as jnp
        import numpy as np
        B, C, H, W = (64, 3, 96, 96)
        P = 16
        HP, WP = (H // P, W // P)
        N = HP * WP
        F = C * P * P
        D = 256
        b = data.shape[0]
        x = data.reshape(b, C, HP, P, WP, P)
        x = x.transpose(0, 2, 4, 1, 3, 5).reshape(b, N, F)
        x = jnp.einsum('bnf,df->bnd', x, W_lin) + b_lin
        cls = jnp.broadcast_to(class_token, (b, 1, D))
        out = jnp.concatenate([cls, x], axis=1) + position_embeddings
        return out

    def _L0_attn_ref(x, W_dq, W_uq, q_ln_g, q_ln_b, W_dkv, W_ukv, kv_ln_g, kv_ln_b, W_o):
        import jax, jax.numpy as jnp
        import numpy as np
        import math
        D_MODEL = 256
        N_HEADS = 16
        Q_PROJ = D_MODEL // 4
        KV_PROJ = D_MODEL // 4
        DH = D_MODEL // N_HEADS
        LN_EPS = 1e-05

        def _layernorm(x, gamma, beta):
            mu = jnp.mean(x, axis=-1, keepdims=True)
            var = jnp.mean(jnp.square(x - mu), axis=-1, keepdims=True)
            return (x - mu) * jax.lax.rsqrt(var + LN_EPS) * gamma + beta
        B, S, D = x.shape
        cq = _layernorm(x @ W_dq, q_ln_g, q_ln_b)
        Q = cq @ W_uq
        ckv = _layernorm(x @ W_dkv, kv_ln_g, kv_ln_b)
        KV = ckv @ W_ukv
        K, V = (KV[..., :D], KV[..., D:])
        q = Q.reshape(B, S, N_HEADS, DH)
        k = K.reshape(B, S, N_HEADS, DH)
        v = V.reshape(B, S, N_HEADS, DH)
        scores = jnp.einsum('bqhd,bkhd->bhqk', q, k) / math.sqrt(float(DH))
        mask = jnp.tril(jnp.ones((S, S), dtype=scores.dtype))
        scores = scores * mask
        scores = jnp.where(scores == 0, -jnp.inf, scores)
        attn = jax.nn.softmax(scores, axis=-1)
        out = jnp.einsum('bhqk,bkhd->bqhd', attn, v).reshape(B, S, D)
        return out @ W_o.T

    def _L0_ffn_ref(x, w12, w3, gate_w):
        import jax, jax.numpy as jnp
        import numpy as np
        TOP_K = 2
        E = gate_w.shape[0]
        H = w3.shape[-1]
        scores = jnp.einsum('btd,ed->bte', x, gate_w)
        topk_scores, topk_idx = jax.lax.top_k(scores, TOP_K)
        topk_probs = jax.nn.softmax(topk_scores, axis=-1)
        total_probs = jnp.sum(jax.nn.one_hot(topk_idx, E, dtype=topk_probs.dtype) * topk_probs[..., None], axis=-2)
        h12 = jnp.einsum('btd,ehd->bteh', x, w12)
        h1, h2 = (h12[..., :H], h12[..., H:])
        hidden = jax.nn.silu(h1) * h2
        expert_out = jnp.einsum('bteh,edh->bted', hidden, w3)
        y = jnp.sum(total_probs[..., None] * expert_out, axis=-2)
        return y
    h = _L0_tok_ref(x, L0_tok_W_lin, L0_tok_b_lin, L0_tok_class_token, L0_tok_position_embeddings)
    h = jnp.concatenate([h, txt], axis=1)
    h = h + _L0_attn_ref(_layernorm(h, axis=-1), L0_attn_W_dq, L0_attn_W_uq, L0_attn_q_ln_g, L0_attn_q_ln_b, L0_attn_W_dkv, L0_attn_W_ukv, L0_attn_kv_ln_g, L0_attn_kv_ln_b, L0_attn_W_o)
    h = h + _L0_ffn_ref(_layernorm(h, axis=-1), L0_ffn_w12, L0_ffn_w3, L0_ffn_gate_w)
    return h

_drawn_inputs = setup_inputs


def setup_inputs(seed=0):
    import zlib

    import numpy as np

    out = dict(_drawn_inputs(seed))
    spreads = {'L0_attn_q_ln_g': (1.0, 0.6),
     'L0_attn_q_ln_b': (0.0, 0.8),
     'L0_attn_kv_ln_g': (1.0, 0.6),
     'L0_attn_kv_ln_b': (0.0, 0.8)}
    factors = {'L0_attn_W_dq': 8.0,
     'L0_attn_W_uq': 8.0,
     'L0_attn_W_dkv': 5.381,
     'L0_attn_W_ukv': 4.059,
     'L0_attn_W_o': 4.355}
    for name, (base, spread) in spreads.items():
        noise = np.random.default_rng([zlib.crc32(name.encode()), seed]).standard_normal(out[name].shape)
        drawn = base * np.exp(spread * noise) if base else spread * noise
        out[name] = jnp.asarray(drawn.astype(out[name].dtype))
    for name, factor in factors.items():
        out[name] = (out[name] * factor).astype(out[name].dtype)
    return out
```

```python
import concourse.bass as bass
from concourse import mybir
from contextlib import ExitStack

P = 128
BATCH, IMG, TXT = 64, 36, 32
S = 1 + IMG + TXT
TOKENS = BATCH * S
D = 256
F = 768
FK = F // P
DK = D // P
IMG_TOKENS = BATCH * IMG
IMG_TILES = IMG_TOKENS // P
HEADS, DH = 16, 16
GROUPS = 4
UNITS = HEADS // GROUPS
PROJ = D // 4
E = 8
TOP = 2
HID = 512
HK = HID // P
TILES = (TOKENS * TOP - E) // P + E
SLOTS = TILES * P
REC = D + 4
REC_ID, REC_SLOT, REC_P1, REC_P2 = D, D + 1, D + 2, D + 3
OUT_ROWS = TOKENS + P
EPS = 1e-5
MASKED = -1e30


def build(nc, patches, txt, w_lin, base_rows, pos, w_down, gamma, beta, w_uq, w_ukv, w_o, w12, w3, gate, out):
    fp32 = mybir.dt.float32
    i32 = mybir.dt.int32
    ALU = mybir.AluOpType
    ACT = mybir.ActivationFunctionType
    AX = mybir.AxisListType

    emb_rows = nc.dram_tensor("emb_rows", [IMG_TOKENS, D], fp32, kind="Internal").ap()
    slot_rows = nc.dram_tensor("slot_rows", [SLOTS, REC], fp32, kind="Internal").ap()

    ctx = ExitStack()
    with ctx:
        sems = {}

        def sem(name):
            sems[name] = ctx.enter_context(nc.semaphore(name))
            return sems[name]

        def sb(stack, name, shape, dt=fp32):
            return stack.enter_context(nc.sbuf_tensor(name, shape, dt))

        def ps(stack, name, shape, dt=fp32):
            return stack.enter_context(nc.psum_tensor(name, shape, dt))

        W12 = sb(ctx, "W12", [P, E * DK * 2 * HID])
        W3 = sb(ctx, "W3", [P, E * HK * D])
        rows = sb(ctx, "rows", [S, BATCH, REC])
        scores_all = sb(ctx, "scores_all", [S, BATCH, E])
        ident = sb(ctx, "ident", [P, P])

        weights_in = sem("weights_in")
        consts_ready = sem("consts_ready")

        embed_and_block(nc, ctx, sb, ps, sem, locals())
        route_and_experts(nc, ctx, sb, ps, sem, locals())


def after(eng, semaphore, value):
    if not (isinstance(value, int) and value <= 0):
        eng.wait_ge(semaphore, value)


def run_steps(eng, body, head, end, total):
    def peeled(n, count):
        body(n, n % 2, lambda k: 0 <= n - k < count)

    for n in range(head):
        peeled(n, total)
    with eng.Fori(0, (end - head) // 2) as i:
        for j in range(2):
            body(i * 2 + (head + j), (head + j) % 2, lambda k: True)
    return peeled


def embed(nc, sb, ps, sem, env):
    ALU, ACT = env["ALU"], env["ACT"]
    patches, out, emb_rows, slot_rows = env["patches"], env["out"], env["emb_rows"], env["slot_rows"]
    W12, W3, ident, weights_in, consts_ready = (env[n] for n in ("W12", "W3", "ident", "weights_in", "consts_ready"))
    base_sb, pos_sb, w_down_sb, gamma_sb, beta_sb = (env[n] for n in ("base_sb", "pos_sb", "w_down_sb", "gamma_sb", "beta_sb"))
    w_qk, w_v, w_o_sb, gate_sb, minus_half, zero_rows = (env[n] for n in ("w_qk", "w_v", "w_o_sb", "gate_sb", "minus_half", "zero_rows"))
    h_in, v_sb, small_in, pads_cleared = (env[n] for n in ("h_in", "v_sb", "small_in", "pads_cleared"))
    with ExitStack() as ctx:
        w_lin_sb = sb(ctx, "w_lin_sb", [P, FK, D])
        patch_sb = [sb(ctx, f"patch_sb{n}", [P, FK, P]) for n in range(2)]
        emb_sb = [sb(ctx, f"emb_sb{n}", [P, D]) for n in range(2)]
        ps_emb = [ps(ctx, f"ps_emb{n}", [P, 512])[:, 0:D] for n in range(2)]
        patch_in = [sem(f"patch_in{n}") for n in range(2)]
        emb_mm = sem("emb_mm")
        emb_copied = sem("emb_copied")
        emb_stored = [sem(f"emb_stored{n}") for n in range(2)]
        zeros_made = sem("zeros_made")
        w_lin_in = sem("w_lin_in")
        block = ctx.enter_context(nc.Block())

        @block.sync
        def _(sp):
            sp.dma_start(w_lin_sb[:, :, :], env["w_lin"].rearrange("(k p) d -> p k d", p=P)).then_inc(w_lin_in, 16)
            for t in range(IMG_TILES):
                if t >= 2:
                    sp.wait_ge(emb_mm, t - 1)
                sp.dma_start(patch_sb[t % 2][:, :, :],
                             patches[:, t * P:(t + 1) * P].rearrange("(k p) n -> p k n", p=P)
                             ).then_inc(patch_in[t % 2], 16)
                if t == 0:
                    sp.dma_start(base_sb[:, :], env["base_rows"]).then_inc(small_in, 16)
                    sp.dma_start(pos_sb[:, :], env["pos"]).then_inc(small_in, 16)
                    sp.dma_start(w_down_sb[:, :, :],
                                 env["w_down"].rearrange("(k p) d -> p k d", p=P)).then_inc(small_in, 16)
                    sp.dma_start(gamma_sb[:, :], env["gamma"]).then_inc(small_in, 16)
                    sp.dma_start(beta_sb[:, :], env["beta"]).then_inc(small_in, 16)
                    sp.wait_ge(zeros_made, 1)
                    spread = w_qk[:, :, :].rearrange("p u (g d) -> p (u g) d", g=GROUPS)
                    sp.dma_start(spread[0:PROJ, :, 0:DH],
                                 env["w_uq"].rearrange("p (h d) -> p h d", d=DH)).then_inc(small_in, 16)
                    sp.dma_start(spread[PROJ:P, :, 0:DH],
                                 env["w_ukv"][:, 0:D].rearrange("p (h d) -> p h d", d=DH)).then_inc(small_in, 16)
                    sp.dma_start(w_v[PROJ:P, :], env["w_ukv"][:, D:2 * D]).then_inc(small_in, 16)
                    sp.dma_start(w_o_sb[:, :, :],
                                 env["w_o"].rearrange("(k p) d -> p k d", p=P)).then_inc(small_in, 16)
                    sp.dma_start(gate_sb[:, :, :],
                                 env["gate"].rearrange("(k p) e -> p k e", p=P)).then_inc(small_in, 16)
            for n in range(2):
                sp.wait_ge(emb_stored[n], 16 * (IMG_TILES // 2))

        @block.gpsimd
        def _(pool):
            pool.memset(w_qk[:, :, :], 0.0).then_inc(zeros_made, 1)
            pool.memset(zero_rows[:, :], 0.0).then_inc(zeros_made, 1)
            pool.memset(minus_half[:, :], -0.5).then_inc(consts_ready, 1)
            for n in range(2):
                pool.memset(v_sb[n][:, :, :], 1.0).then_inc(consts_ready, 1)
            pool.memset(ident[:, :], 0.0).then_inc(consts_ready, 1)
            pool.wait_ge(consts_ready, 4)
            pool.affine_select(out=ident[:, :], in_=ident[:, :], compare_op=ALU.not_equal, fill=1.0, base=0,
                               pattern=[[-1, P]], channel_multiplier=1).then_inc(consts_ready, 1)
            pool.wait_ge(zeros_made, 2)
            for t in range(0, TILES, 4):
                pool.dma_start(slot_rows[t * P:(t + 4) * P, :].rearrange("(n p) c -> p n c", p=P),
                               zero_rows[:, :].unsqueeze(1).to_broadcast([P, 4, REC])).then_inc(pads_cleared, 16)
            pool.dma_start(out[TOKENS:OUT_ROWS, :], zero_rows[:, 0:D]).then_inc(pads_cleared, 16)

        @block.scalar
        def _(act):
            for e in range(E):
                act.dma_start(W12[:, e * DK * 2 * HID:(e + 1) * DK * 2 * HID].rearrange("p (k h) -> p k h", k=DK),
                              env["w12"][e].rearrange("(k p) h -> p k h", p=P)).then_inc(weights_in, 16)
                act.dma_start(W3[:, e * HK * D:(e + 1) * HK * D].rearrange("p (c d) -> p c d", c=HK),
                              env["w3"][e].rearrange("(c p) d -> p c d", p=P)).then_inc(weights_in, 16)
            for t in range(IMG_TILES):
                act.wait_ge(emb_mm, t + 1)
                if t >= 2:
                    act.wait_ge(emb_stored[t % 2], 16 * (t // 2))
                act.activation(emb_sb[t % 2][:, :], ps_emb[t % 2], ACT.Copy).then_inc(emb_copied, 1)
                act.wait_ge(emb_copied, t + 1)
                act.dma_start(emb_rows[t * P:(t + 1) * P, :], emb_sb[t % 2][:, :]).then_inc(emb_stored[t % 2], 16)


        @block.tensor
        def _(pe):
            pe.wait_ge(consts_ready, 5)
            pe.wait_ge(w_lin_in, 16)
            for t in range(IMG_TILES):
                pe.wait_ge(patch_in[t % 2], 16 * (t // 2 + 1))
                if t >= 2:
                    pe.wait_ge(emb_copied, t - 1)
                for k in range(FK):
                    mm = pe.matmul(ps_emb[t % 2], patch_sb[t % 2][:, k, :], w_lin_sb[:, k, :],
                                   start=(k == 0), stop=(k == FK - 1))
                mm.then_inc(emb_mm, 1)



def embed_and_block(nc, outer, sb, ps, sem, env):
    fp32, ALU, ACT, AX = env["fp32"], env["ALU"], env["ACT"], env["AX"]
    patches, txt, out = env["patches"], env["txt"], env["out"]
    emb_rows, slot_rows = env["emb_rows"], env["slot_rows"]
    W12, W3, rows, scores_all, ident = (env[n] for n in ("W12", "W3", "rows", "scores_all", "ident"))
    weights_in, consts_ready = env["weights_in"], env["consts_ready"]

    ctx = ExitStack()
    with ctx:
        base_sb = sb(ctx, "base_sb", [1 + IMG, D])
        pos_sb = sb(ctx, "pos_sb", [1 + IMG, D])
        w_down_sb = sb(ctx, "w_down_sb", [P, DK, P])
        gamma_sb = sb(ctx, "gamma_sb", [P, 1])
        beta_sb = sb(ctx, "beta_sb", [P, 1])
        w_qk = sb(ctx, "w_qk", [P, UNITS, P])
        w_v = sb(ctx, "w_v", [P, D])
        w_o_sb = sb(ctx, "w_o_sb", [P, DK, D])
        gate_sb = sb(ctx, "gate_sb", [P, DK, E])
        minus_half = sb(ctx, "minus_half", [S, 2])
        zero_rows = sb(ctx, "zero_rows", [P, REC])

        small_in = sem("small_in")
        pads_cleared = sem("pads_cleared")
        h_in = [sb(ctx, f"h_in{n}", [S, D]) for n in range(2)]
        v_sb = [sb(ctx, f"v_sb{n}", [S, HEADS, DH + 1]) for n in range(2)]
        embed(nc, sb, ps, sem, {**env, **locals()})

        stats1 = sb(ctx, "stats1", [S, 6])
        mv1 = sb(ctx, "mv1", [S, 2])
        rstd1 = sb(ctx, "rstd1", [S, 1])
        xn = sb(ctx, "xn", [S, D])
        xn_t = sb(ctx, "xn_t", [P, DK, S])
        stats_c = sb(ctx, "stats_c", [S, 2, 6])
        mv_c = sb(ctx, "mv_c", [S, 2, 2])
        rstd_c = sb(ctx, "rstd_c", [S, 2])
        cn = sb(ctx, "cn", [S, P])
        c_t = [sb(ctx, f"c_t{n}", [P, S]) for n in range(2)]
        q_t = sb(ctx, "q_t", [P, UNITS, S])
        k_t = sb(ctx, "k_t", [P, UNITS, S])
        probs = [sb(ctx, f"probs{n}", [S, HEADS, S]) for n in range(2)]
        zeros_out = sb(ctx, "zeros_out", [S, HEADS, S])
        row_max = sb(ctx, "row_max", [S, HEADS])
        p_t = [sb(ctx, f"p_t{n}", [S, UNITS * S]) for n in range(2)]
        inv_sum = sb(ctx, "inv_sum", [S, HEADS])
        o_norm = sb(ctx, "o_norm", [S, HEADS, DH])
        o_t = sb(ctx, "o_t", [P, DK, S])
        h_out = [sb(ctx, f"h_out{n}", [S, D]) for n in range(2)]
        stats2 = sb(ctx, "stats2", [S, 6])
        mv2 = sb(ctx, "mv2", [S, 2])
        rstd2 = sb(ctx, "rstd2", [S, 1])
        xn2 = sb(ctx, "xn2", [S, D])
        xn2_t = sb(ctx, "xn2_t", [P, DK, S])

        ps_scores = ps(ctx, "ps_scores", [P, GROUPS, 512])
        ps_pt = [ps(ctx, f"ps_pt{n}", [P, 512]) for n in range(2)]
        ps_in = ps(ctx, "ps_in", [P, 512])
        ps_out = ps(ctx, "ps_out", [P, 512])
        ps_xt = ps_in[:, 0:DK * S].rearrange("p (k s) -> p k s", k=DK)
        ps_down = ps_in[0:S, 144:144 + P]
        ps_ct = ps_in[:, 280:280 + S]
        ps_o = ps_out[0:S, 0:HEADS * (DH + 1)].rearrange("p (h d) -> p h d", h=HEADS)
        ps_ot = ps_out[:, 0:DK * S].rearrange("p (k s) -> p k s", k=DK)
        ps_wo = ps_out[0:S, 144:144 + D]
        ps_x2t = ps_scores[:, 3, 0:DK * S].rearrange("p (k s) -> p k s", k=DK)
        ps_gate = ps_scores[0:S, 3, 144:144 + E]

        base_ready = sem("base_ready")
        loaded = [sem(f"loaded{n}") for n in range(2)]
        h_ready = sem("h_ready")
        h_kept = sem("h_kept")
        stats1_done, mv1_done, rstd1_done = sem("stats1_done"), sem("mv1_done"), sem("rstd1_done")
        xn_ready = sem("xn_ready")
        xt_done, xt_copied = sem("xt_done"), sem("xt_copied")
        down_done = sem("down_done")
        stats_c_done, mv_c_done, rstd_c_done = sem("stats_c_done"), sem("mv_c_done"), sem("rstd_c_done")
        cn_ready = sem("cn_ready")
        ct_done, ct_copied = sem("ct_done"), sem("ct_copied")
        qk_done, qk_copied = sem("qk_done"), sem("qk_copied")
        v_done, v_copied = sem("v_done"), sem("v_copied")
        scores_done, scores_copied = sem("scores_done"), sem("scores_copied")
        causal_done = sem("causal_done")
        zero_marked, zero_masked, max_done, shifted, exp_done = (
            sem("zero_marked"), sem("zero_masked"), sem("max_done"), sem("shifted"), sem("exp_done"))
        pt_done, pt_copied, pv_unit = sem("pt_done"), sem("pt_copied"), sem("pv_unit")
        inv_done, o_ready = sem("inv_done"), sem("o_ready")
        ot_done, ot_copied, wo_done = sem("ot_done"), sem("ot_copied"), sem("wo_done")
        h_out_ready = sem("h_out_ready")
        h_stored = [sem(f"h_stored{n}") for n in range(2)]
        stats2_done, mv2_done, rstd2_done = sem("stats2_done"), sem("mv2_done"), sem("rstd2_done")
        aggr1, aggr2, aggr_c = sem("aggr1"), sem("aggr2"), sem("aggr_c")
        xn2_ready, row_kept = sem("xn2_ready"), sem("row_kept")
        x2t_done, x2t_copied, gate_done, gate_copied = (
            sem("x2t_done"), sem("x2t_copied"), sem("gate_done"), sem("gate_copied"))

        HEAD, END, ALL = 8, BATCH, BATCH + 5
        SMALL = 10

        block = ctx.enter_context(nc.Block())

        @block.sync
        def _(sp):
            def load(b, par):
                after(sp, xn_ready, b - 1)
                after(sp, h_kept, b - 1)
                if isinstance(b, int):
                    img, text = emb_rows[b * IMG:(b + 1) * IMG, :], txt[b * TXT:(b + 1) * TXT, :]
                else:
                    img, text = emb_rows[bass.ds(b * IMG, IMG), :], txt[bass.ds(b * TXT, TXT), :]
                sp.dma_start(h_in[par][0:1, :], zero_rows[0:1, 0:D]).then_inc(loaded[par], 16)
                sp.dma_start(h_in[par][1:1 + IMG, :], img).then_inc(loaded[par], 16)
                sp.dma_start(h_in[par][1 + IMG:S, :], text).then_inc(loaded[par], 16)

            def store(b, par):
                sp.wait_ge(h_out_ready, b + 1)
                dst = out[b * S:(b + 1) * S, :] if isinstance(b, int) else out[bass.ds(b * S, S), :]
                sp.dma_start(dst, h_out[par][:, :]).then_inc(h_stored[par], 16)

            def body(s, par, active):
                if active(0):
                    load(s, par)
                if active(4):
                    store(s - 4, par)

            peeled = run_steps(sp, body, HEAD, END, BATCH)
            for s in range(END, ALL):
                peeled(s, BATCH)
            for n in range(2):
                sp.wait_ge(h_stored[n], 16 * (BATCH // 2))
            sp.wait_ge(pads_cleared, 16 * (TILES // 4 + 1))

        @block.gpsimd
        def _(pool):
            masked = pool.to_reg(MASKED)

            def body(s, par, active):
                if active(0):
                    pool.wait_ge(mv1_done, s + 1)
                    after(pool, xn_ready, s)
                    pool.tensor_tensor(rstd1[:, :], mv1[:, 1:2], minus_half[:, 0:1], ALU.pow).then_inc(rstd1_done, 1)
                    pool.wait_ge(h_ready, s + 1)
                    pool.tensor_copy(batch_rows(s), h_in[par][:, :].unsqueeze(1)).then_inc(h_kept, 1)
                if active(2):
                    copied = s - 1 if isinstance(s, int) else pool.to_reg(s - 1)
                    pool.wait_ge(consts_ready, 5)
                    pool.wait_ge(scores_copied, copied)
                    pr = probs[par]
                    pool.affine_select(out=pr[:, :, :], in_=pr[:, :, :], compare_op=ALU.is_ge, fill=masked, base=0,
                                       pattern=[[0, HEADS], [-1, S]], channel_multiplier=1).then_inc(causal_done, 1)
                if active(4):
                    pool.wait_ge(mv2_done, s - 3)
                    after(pool, xn2_ready, s - 4)
                    pool.tensor_tensor(rstd2[:, :], mv2[:, 1:2], minus_half[:, 0:1], ALU.pow).then_inc(rstd2_done, 1)
                if active(0):
                    pool.wait_ge(mv_c_done, s + 1)
                    after(pool, cn_ready, s)
                    pool.tensor_tensor(rstd_c[:, :], mv_c[:, :, 1], minus_half[:, :], ALU.pow).then_inc(rstd_c_done, 1)
                if active(4):
                    pool.wait_ge(xn2_ready, s - 3)
                    pool.tensor_copy(batch_rows(s - 4), xn2[:, :].unsqueeze(1)).then_inc(row_kept, 1)

            def batch_rows(b):
                return rows[:, b:b + 1, 0:D] if isinstance(b, int) else rows[:, bass.ds(b, 1), 0:D]

            peeled = run_steps(pool, body, HEAD, END, BATCH)
            for s in range(END, ALL):
                peeled(s, BATCH)

        @block.scalar
        def _(act):
            def body(s, par, active):
                if active(2):
                    act.wait_ge(scores_done, s - 1)
                    after(act, pt_done, (s - 3) * UNITS)
                    act.activation(probs[par][:, :, :].rearrange("p (g u) s -> p g (u s)", g=GROUPS),
                                   ps_scores[0:S, :, 0:UNITS * S], ACT.Copy).then_inc(scores_copied, 1)
                if active(4):
                    act.wait_ge(ot_done, s - 3)
                    act.activation(o_t[:, :, :], ps_ot, ACT.Copy).then_inc(ot_copied, 1)
                if active(0):
                    act.wait_ge(xt_done, s + 1)
                    act.activation(xn_t[:, :, :], ps_xt, ACT.Copy).then_inc(xt_copied, 1)

                def copy_turned(u):
                    n = (s - 3) * UNITS + u
                    act.wait_ge(pt_done, n + 1)
                    after(act, pv_unit, n - 1)
                    act.activation(p_t[u % 2][:, :], ps_pt[u % 2][0:S, 0:UNITS * S], ACT.Copy).then_inc(pt_copied, 1)

                if active(3):
                    copy_turned(0)
                    copy_turned(1)
                if active(5):
                    act.wait_ge(x2t_done, s - 4)
                    act.activation(xn2_t[:, :, :], ps_x2t, ACT.Copy).then_inc(x2t_copied, 1)
                if active(3):
                    copy_turned(2)
                    copy_turned(3)
                if active(1):
                    act.wait_ge(qk_done, s)
                    after(act, scores_done, s - 1)
                    act.activation(q_t[:, :, :], ps_scores[:, 0, 0:UNITS * S].rearrange("p (u s) -> p u s", u=UNITS),
                                   ACT.Copy)
                    act.activation(k_t[:, :, :], ps_scores[:, 1, 0:UNITS * S].rearrange("p (u s) -> p u s", u=UNITS),
                                   ACT.Copy).then_inc(qk_copied, 1)
                if active(2):
                    act.wait_ge(v_done, s - 1)
                    after(act, pv_unit, (s - 3) * UNITS)
                    act.activation(v_sb[par][:, :, 0:DH], ps_scores[0:S, 2, 0:D].rearrange("p (h d) -> p h d", h=HEADS),
                                   ACT.Copy).then_inc(v_copied, 1)
                    act.wait_ge(shifted, s - 1)
                    act.activation(probs[par][:, :, :], probs[par][:, :, :], ACT.Exp,
                                   scale=float(DH) ** -0.5).then_inc(exp_done, 1)
                if active(0):
                    act.wait_ge(ct_done, s + 1)
                    after(act, v_done, s - 1)
                    act.activation(c_t[par][:, :], ps_ct, ACT.Identity, bias=beta_sb[:, 0:1],
                                   scale=gamma_sb[:, 0:1]).then_inc(ct_copied, 1)

            peeled = run_steps(act, body, HEAD, END, BATCH)
            for s in range(END, ALL):
                peeled(s, BATCH)

        @block.tensor
        def _(pe):
            def body(s, par, active):
                if active(2):
                    pe.wait_ge(qk_copied, s - 1)
                    after(pe, v_copied, s - 2)
                    after(pe, gate_copied, s - 5)
                    for u in range(UNITS):
                        for g in range(GROUPS):
                            mm = pe.matmul(ps_scores[0:S, g, u * S:(u + 1) * S], q_t[32 * g:32 * g + DH, u, :],
                                           k_t[32 * g:32 * g + DH, u, :], start=True, stop=True)
                    mm.then_inc(scores_done, 1)
                if active(4):
                    pe.wait_ge(o_ready, s - 3)
                    for k in range(DK):
                        mm = pe.transpose(ps_ot[:, k, :],
                                          o_norm[:, k * (P // DH):(k + 1) * (P // DH), :].rearrange("p h d -> p (h d)"),
                                          ident[0:S, 0:S])
                    mm.then_inc(ot_done, 1)
                if active(0):
                    pe.wait_ge(xn_ready, s + 1)
                    after(pe, ct_copied, s)
                    for k in range(DK):
                        mm = pe.transpose(ps_xt[:, k, :], xn[:, k * P:(k + 1) * P], ident[0:S, 0:S])
                    mm.then_inc(xt_done, 1)

                def turn(u):
                    n = (s - 3) * UNITS + u
                    if u == 0:
                        pe.wait_ge(exp_done, s - 2)
                    after(pe, pt_copied, n - 1)
                    for g in range(GROUPS):
                        mm = pe.transpose(ps_pt[u % 2][0:S, g * S:(g + 1) * S], probs[1 - par][:, g * UNITS + u, :],
                                          ident[0:S, 0:S])
                    mm.then_inc(pt_done, 1)

                def times_v(u):
                    n = (s - 3) * UNITS + u
                    if u == 0:
                        pe.wait_ge(v_copied, s - 2)
                        after(pe, h_out_ready, s - 3)
                    pe.wait_ge(pt_copied, n + 1)
                    for g in range(GROUPS):
                        mm = pe.matmul(ps_o[:, u * GROUPS + g, :], p_t[u % 2][:, g * S:(g + 1) * S],
                                       v_sb[1 - par][:, u * GROUPS + g, :], start=True, stop=True)
                    mm.then_inc(pv_unit, 1)

                if active(3):
                    turn(0)
                    turn(1)
                if active(4):
                    pe.wait_ge(ot_copied, s - 3)
                    for k in range(DK):
                        mm = pe.matmul(ps_wo, o_t[:, k, :], w_o_sb[:, k, :], start=(k == 0), stop=(k == DK - 1))
                    mm.then_inc(wo_done, 1)
                if active(5):
                    pe.wait_ge(xn2_ready, s - 4)
                    after(pe, scores_copied, min(s - 1, BATCH) if isinstance(s, int) else s - 1)
                    if isinstance(s, int) and s >= BATCH + 2:
                        pe.wait_ge(gate_copied, s - 5)
                    for k in range(DK):
                        mm = pe.transpose(ps_x2t[:, k, :], xn2[:, k * P:(k + 1) * P], ident[0:S, 0:S])
                    mm.then_inc(x2t_done, 1)
                if active(0):
                    pe.wait_ge(xt_copied, s + 1)
                    for k in range(DK):
                        mm = pe.matmul(ps_down, xn_t[:, k, :], w_down_sb[:, k, :], start=(k == 0), stop=(k == DK - 1))
                    mm.then_inc(down_done, 1)
                if active(3):
                    times_v(0)
                    turn(2)
                    times_v(1)
                    turn(3)
                if active(1):
                    pe.wait_ge(ct_copied, s)
                    after(pe, scores_copied, s - 1)
                    ct = c_t[1 - par]
                    for u in range(UNITS):
                        pe.matmul(ps_scores[:, 0, u * S:(u + 1) * S], w_qk[0:PROJ, u, :], ct[0:PROJ, :],
                                  start=True, stop=True)
                        mm = pe.matmul(ps_scores[:, 1, u * S:(u + 1) * S], w_qk[PROJ:P, u, :], ct[PROJ:P, :],
                                       start=True, stop=True)
                    mm.then_inc(qk_done, 1)
                if active(3):
                    times_v(2)
                    times_v(3)
                if active(2):
                    pe.wait_ge(scores_copied, s - 1)
                    pe.matmul(ps_scores[0:S, 2, 0:D], c_t[par][PROJ:P, :], w_v[PROJ:P, :],
                              start=True, stop=True).then_inc(v_done, 1)
                if active(5):
                    pe.wait_ge(x2t_copied, s - 4)
                    for k in range(DK):
                        mm = pe.matmul(ps_gate, xn2_t[:, k, :], gate_sb[:, k, :], start=(k == 0), stop=(k == DK - 1))
                    mm.then_inc(gate_done, 1)
                if active(0):
                    pe.wait_ge(cn_ready, s + 1)
                    pe.transpose(ps_ct, cn[:, :], ident[0:S, 0:S]).then_inc(ct_done, 1)

            peeled = run_steps(pe, body, HEAD, END, BATCH)
            for s in range(END, ALL):
                peeled(s, BATCH)

        @block.vector
        def _(dve):
            dve.wait_ge(small_in, 16 * SMALL)
            dve.tensor_tensor(base_sb[:, :], base_sb[:, :], pos_sb[:, :], ALU.add).then_inc(base_ready, 1)
            dve.wait_ge(base_ready, 1)

            def body(s, par, active):
                if active(4):
                    dve.wait_ge(pv_unit, (s - 3) * UNITS)
                    dve.reciprocal(inv_sum[:, :], ps_o[:, :, DH]).then_inc(inv_done, 1)
                if active(0):
                    dve.wait_ge(loaded[par], 48 * (s // 2 + 1) if isinstance(s, int) else (s - par + 2) * 24)
                    h = h_in[par]
                    dve.tensor_tensor(h[0:1 + IMG, :], h[0:1 + IMG, :], base_sb[:, :], ALU.add).then_inc(h_ready, 1)
                if active(0):
                    dve.wait_ge(h_ready, s + 1)
                    dve.bn_stats(stats1[:, :], h_in[par][:, :]).then_inc(stats1_done, 1)
                    dve.wait_ge(stats1_done, s + 1)
                if active(4):
                    dve.wait_ge(inv_done, s - 3)
                    dve.tensor_tensor(o_norm[:, :, :], ps_o[:, :, 0:DH],
                                      inv_sum[:, :].unsqueeze(2).to_broadcast([S, HEADS, DH]),
                                      ALU.mult).then_inc(o_ready, 1)
                if active(0):
                    dve.bn_aggr(mv1[:, :], stats1[:, :]).then_inc(aggr1, 1)
                    dve.wait_ge(aggr1, s + 1)
                    dve.tensor_scalar(mv1[:, 1:2], mv1[:, 1:2], EPS, None, ALU.add).then_inc(mv1_done, 1)
                    dve.wait_ge(rstd1_done, s + 1)
                    after(dve, xt_done, s)
                    dve.tensor_scalar(xn[:, :], h_in[par][:, :], mv1[:, 0:1], rstd1[:, 0:1], ALU.subtract,
                                      ALU.mult).then_inc(xn_ready, 1)
                if active(4):
                    b = s - 4
                    dve.wait_ge(wo_done, b + 1)
                    after(dve, h_stored[par], 16 * (b // 2) if isinstance(b, int) else (b - par) * 8)
                    hs = (rows[:, b, 0:D] if isinstance(b, int)
                          else rows[:, bass.ds(b, 1), 0:D].rearrange("p a d -> p (a d)"))
                    dve.tensor_tensor(h_out[par][:, :], ps_wo, hs, ALU.add).then_inc(h_out_ready, 1)
                    dve.wait_ge(h_out_ready, b + 1)
                    dve.bn_stats(stats2[:, :], h_out[par][:, :]).then_inc(stats2_done, 1)
                    dve.wait_ge(stats2_done, b + 1)
                if active(2):
                    dve.wait_ge(causal_done, s - 1)
                    dve.tensor_scalar(zeros_out[:, :, :], probs[par][:, :, :], 0.0, MASKED, ALU.is_equal,
                                      ALU.mult).then_inc(zero_marked, 1)
                if active(4):
                    dve.bn_aggr(mv2[:, :], stats2[:, :]).then_inc(aggr2, 1)
                    dve.wait_ge(aggr2, s - 3)
                    dve.tensor_scalar(mv2[:, 1:2], mv2[:, 1:2], EPS, None, ALU.add).then_inc(mv2_done, 1)
                if active(0):
                    dve.wait_ge(down_done, s + 1)
                    for n in range(2):
                        stat = dve.bn_stats(stats_c[:, n, :], ps_down[:, n * PROJ:(n + 1) * PROJ])
                    stat.then_inc(stats_c_done, 1)
                    dve.wait_ge(stats_c_done, s + 1)
                if active(2):
                    dve.wait_ge(zero_marked, s - 1)
                    dve.tensor_tensor(probs[par][:, :, :], probs[par][:, :, :], zeros_out[:, :, :],
                                      ALU.add).then_inc(zero_masked, 1)
                if active(0):
                    for n in range(2):
                        stat = dve.bn_aggr(mv_c[:, n, :], stats_c[:, n, :])
                    stat.then_inc(aggr_c, 1)
                    dve.wait_ge(aggr_c, s + 1)
                    dve.tensor_scalar(mv_c[:, :, 1], mv_c[:, :, 1], EPS, None, ALU.add).then_inc(mv_c_done, 1)
                if active(2):
                    dve.wait_ge(zero_masked, s - 1)
                    dve.tensor_reduce(row_max[:, :], probs[par][:, :, :], AX.X, ALU.max).then_inc(max_done, 1)
                if active(0):
                    dve.wait_ge(rstd_c_done, s + 1)
                    after(dve, ct_done, s)
                    for n in range(2):
                        last = dve.tensor_scalar(cn[:, n * PROJ:(n + 1) * PROJ],
                                                 ps_down[:, n * PROJ:(n + 1) * PROJ], mv_c[:, n, 0:1],
                                                 rstd_c[:, n:n + 1], ALU.subtract, ALU.mult)
                    last.then_inc(cn_ready, 1)
                if active(2):
                    dve.wait_ge(max_done, s - 1)
                    dve.tensor_tensor(probs[par][:, :, :], probs[par][:, :, :],
                                      row_max[:, :].unsqueeze(2).to_broadcast([S, HEADS, S]),
                                      ALU.subtract).then_inc(shifted, 1)
                if active(4):
                    dve.wait_ge(rstd2_done, s - 3)
                    after(dve, x2t_done, s - 4)
                    after(dve, row_kept, s - 4)
                    dve.tensor_scalar(xn2[:, :], h_out[par][:, :], mv2[:, 0:1], rstd2[:, 0:1], ALU.subtract,
                                      ALU.mult).then_inc(xn2_ready, 1)
                if active(5):
                    b = s - 5
                    dve.wait_ge(gate_done, b + 1)
                    dst = (scores_all[:, b, :] if isinstance(b, int)
                           else scores_all[:, bass.ds(b, 1), :].rearrange("p a e -> p (a e)"))
                    dve.tensor_copy(dst, ps_gate).then_inc(gate_copied, 1)

            peeled = run_steps(dve, body, HEAD, END, BATCH)
            for s in range(END, ALL):
                peeled(s, BATCH)


def route_and_experts(nc, outer, sb, ps, sem, env):
    fp32, i32, ALU, ACT, AX = env["fp32"], env["i32"], env["ALU"], env["ACT"], env["AX"]
    out, slot_rows = env["out"], env["slot_rows"]
    W12, W3, rows, scores_all, ident = (env[n] for n in ("W12", "W3", "rows", "scores_all", "ident"))
    weights_in = env["weights_in"]

    ctx = ExitStack()
    with ctx:
        tie_rank = sb(ctx, "tie_rank", [S, E])
        before = sb(ctx, "before", [S, S])
        ones = sb(ctx, "ones", [S, S])
        iota_i = sb(ctx, "iota_i", [P, P], i32)
        token_i = sb(ctx, "token_i", [S, BATCH], i32)
        first = [sb(ctx, f"first{n}", [S, BATCH, E]) for n in range(TOP)]
        work = sb(ctx, "work", [S, BATCH, E])
        work2 = sb(ctx, "work2", [S, BATCH, E])
        rest = sb(ctx, "rest", [S, BATCH, E])
        top = [sb(ctx, f"top{n}", [S, BATCH]) for n in range(TOP)]
        small = sb(ctx, "small", [S, BATCH])
        both = sb(ctx, "both", [S, BATCH, E])
        running = sb(ctx, "running", [S, BATCH, E])
        count_i = sb(ctx, "count_i", [S, E], i32)
        tiles_f = sb(ctx, "tiles_f", [S, E])
        tile_end = sb(ctx, "tile_end", [S, E])
        tile_start = sb(ctx, "tile_start", [S, E])
        slot_f = sb(ctx, "slot_f", [S, TOP, BATCH])
        slot_i = sb(ctx, "slot_i", [S, TOP, BATCH], i32)
        tile_no = sb(ctx, "tile_no", [1, TILES])
        tile_expert = sb(ctx, "tile_expert", [1, TILES])
        tile_expert_i = sb(ctx, "tile_expert_i", [1, TILES], i32)
        trash_row = sb(ctx, "trash_row", [P, 1])
        my_slot = [sb(ctx, f"my_slot{n}", [P, 1]) for n in range(2)]

        x_in = [sb(ctx, f"x_in{n}", [P, REC]) for n in range(2)]
        x_t = [sb(ctx, f"x_t{n}", [P, DK, P]) for n in range(2)]
        gated = sb(ctx, "gated", [P, HID])
        hidden = [sb(ctx, f"hidden{n}", [P, HID]) for n in range(2)]
        hidden_t = [sb(ctx, f"hidden_t{n}", [P, HK, P]) for n in range(1)]
        y_sb = [sb(ctx, f"y_sb{n}", [P, D]) for n in range(2)]
        is_first = sb(ctx, "is_first", [P, 1])
        second_p = sb(ctx, "second_p", [P, 1])
        weight = [sb(ctx, f"weight{n}", [P, 1]) for n in range(2)]
        pad_row = sb(ctx, "pad_row", [P, 1])
        dest = [sb(ctx, f"dest{n}", [P, 1], i32) for n in range(2)]

        ps_xt = ps(ctx, "ps_xt_moe", [P, DK, P])
        ps_h = [ps(ctx, f"ps_h{n}", [P, 2, HID]) for n in range(2)]
        ps_ht = ps(ctx, "ps_ht", [P, HK, P])
        ps_y = ps(ctx, "ps_y", [P, 512])
        ps_prefix = ps_h[0][0:S, 0, :]
        ps_total = ps_h[0][0:S, 1, :]

        made = sem("route_consts")
        chain = sem("route_chain")
        both_ready, prefix_done = sem("both_ready"), sem("prefix_done")
        gap_ready, gap_exp = sem("gap_ready"), sem("gap_exp")
        slots_ready, tile_expert_ready = sem("slots_ready"), sem("tile_expert_ready")
        scattered = sem("scattered")
        x_loaded = [sem(f"x_loaded{n}") for n in range(2)]
        xt_done, xt_copied = sem("moe_xt_done"), sem("moe_xt_copied")
        h_done, silu_done, hidden_ready = sem("h_done"), sem("silu_done"), sem("hidden_ready")
        ht_done, ht_copied = sem("ht_done"), sem("ht_copied")
        y_done, y_ready = sem("y_done"), sem("y_ready")
        first_known, second_known, weight_known, pad_known, dest_known, slot_moved = (
            sem("first_known"), sem("second_known"), sem("weight_known"), sem("pad_known"), sem("dest_known"),
            sem("slot_moved"))
        y_added = sem("y_added")

        HEAD, END, ALL = 4, TILES, TILES + 2
        block = ctx.enter_context(nc.Block())

        @block.gpsimd
        def _(pool):
            pool.iota(token_i[:, :], pattern=[[S, BATCH]], base=1, channel_multiplier=1).then_inc(made, 1)
            pool.iota(iota_i[:, 0:E], pattern=[[-1, E]], base=E, channel_multiplier=0).then_inc(made, 1)
            pool.iota(iota_i[:, E:E + TILES], pattern=[[1, TILES]], base=0, channel_multiplier=0).then_inc(made, 1)
            pool.iota(iota_i[:, P - 1:P], pattern=[[0, 1]], base=0, channel_multiplier=1).then_inc(made, 1)
            pool.memset(ones[:, :], 1.0).then_inc(made, 1)
            pool.wait_ge(made, 5)
            pool.affine_select(out=before[:, :], in_=ones[:, :], compare_op=ALU.is_gt, fill=0.0, base=0,
                               pattern=[[1, S]], channel_multiplier=-1).then_inc(made, 1)
            pool.wait_ge(slots_ready, 1)
            for b in range(BATCH):
                for n in range(TOP):
                    pool.indirect_dma_start(
                        out=slot_rows[:, :], out_offset=bass.IndirectOffsetOnAxis(ap=slot_i[:, n, b:b + 1], axis=0),
                        in_=rows[:, b, :], in_offset=None, bounds_check=SLOTS - 1).then_inc(scattered, 16)

            last_row = pool.to_reg(OUT_ROWS - 1)

            def body(s, par, active):
                if active(2):
                    t = s - 2
                    added = 16 * t if isinstance(t, int) else pool.to_reg(t * 16)
                    done = t + 1 if isinstance(t, int) else pool.to_reg(t + 1)
                    pool.wait_ge(slots_ready, 1)
                    after(pool, y_added, added)
                    pool.wait_ge(y_ready, done)
                    pool.wait_ge(dest_known, done)
                    pool.indirect_dma_start(
                        out=out[:, :], out_offset=bass.IndirectOffsetOnAxis(ap=dest[par][:, 0:1], axis=0),
                        in_=y_sb[par][:, :], in_offset=None, bounds_check=last_row,
                        compute_op=ALU.add).then_inc(y_added, 16)

            peeled = run_steps(pool, body, HEAD, END, TILES)
            for s in range(END, ALL):
                peeled(s, TILES)
            pool.wait_ge(y_added, 16 * TILES)

        @block.sync
        def _(sp):
            sp.wait_ge(scattered, 16 * BATCH * TOP)

            def body(s, par, active):
                if active(0):
                    after(sp, xt_done, s - 1)
                    after(sp, dest_known, s - 1)
                    after(sp, weight_known, s - 1)
                    src = slot_rows[s * P:(s + 1) * P, :] if isinstance(s, int) else slot_rows[bass.ds(s * P, P), :]
                    sp.dma_start(x_in[par][:, :], src).then_inc(x_loaded[par], 16)

            peeled = run_steps(sp, body, HEAD, END, TILES)

        @block.vector
        def _(dve):
            links = [0]

            def link(ins):
                links[0] += 1
                ins.then_inc(chain, 1)
                dve.wait_ge(chain, links[0])

            def per_expert(ap):
                return ap.unsqueeze(2).to_broadcast([S, BATCH, E])

            dve.wait_ge(made, 6)
            link(dve.tensor_copy(tie_rank[:, :], iota_i[0:S, 0:E]))
            link(dve.tensor_copy(tile_no[:, :], iota_i[0:1, E:E + TILES]))
            link(dve.tensor_scalar(trash_row[:, :], iota_i[:, P - 1:P], float(TOKENS + 1), None, ALU.add))
            for n in range(2):
                link(dve.tensor_scalar(my_slot[n][:, :], iota_i[:, P - 1:P], float(n * P), None, ALU.add))

            ranks = tie_rank[:, :].unsqueeze(1).to_broadcast([S, BATCH, E])
            scores = scores_all
            for n in range(TOP):
                link(dve.tensor_reduce(top[n][:, :], scores[:, :, :], AX.X, ALU.max))
                link(dve.tensor_tensor(work[:, :, :], scores[:, :, :], per_expert(top[n][:, :]), ALU.is_equal))
                link(dve.tensor_tensor(work[:, :, :], work[:, :, :], ranks, ALU.mult))
                link(dve.tensor_reduce(small[:, :], work[:, :, :], AX.X, ALU.max))
                link(dve.tensor_tensor(first[n][:, :, :], work[:, :, :], per_expert(small[:, :]), ALU.is_equal))
                if n == 0:
                    link(dve.scalar_tensor_tensor(rest[:, :, :], first[0][:, :, :], MASKED, scores_all[:, :, :],
                                                  ALU.mult, ALU.add))
                    scores = rest
            dve.tensor_tensor(both[:, :, :], first[0][:, :, :], first[1][:, :, :], ALU.add).then_inc(both_ready, 1)
            dve.tensor_tensor(small[:, :], top[1][:, :], top[0][:, :], ALU.subtract).then_inc(gap_ready, 1)
            dve.wait_ge(gap_exp, 1)
            link(dve.tensor_scalar(top[0][:, :], small[:, :], 1.0, None, ALU.add))
            link(dve.reciprocal(top[1][:, :], top[0][:, :]))
            link(dve.tensor_copy(rows[:, :, REC_P1], top[1][:, :]))
            link(dve.tensor_tensor(rows[:, :, REC_P2], top[1][:, :], small[:, :], ALU.mult))
            link(dve.tensor_copy(rows[:, :, REC_ID], token_i[:, :]))

            dve.wait_ge(prefix_done, 1)
            link(dve.tensor_copy(work[:, :, :], ps_total.rearrange("p (b e) -> p b e", e=E)))
            for e in range(E):
                link(dve.tensor_tensor_scan(running[:, :, e], work[:, :, e], work[:, :, e], 0.0, ALU.bypass, ALU.add)
                     if False else dve.tensor_tensor_scan(running[:, :, e], ones[:, 0:BATCH], work[:, :, e], 0.0,
                                                          ALU.mult, ALU.add))
            link(dve.tensor_scalar(count_i[:, :], running[:, BATCH - 1, :], float(P - 1), None, ALU.add))
            link(dve.tensor_scalar(count_i[:, :], count_i[:, :], P.bit_length() - 1, None, ALU.arith_shift_right))
            link(dve.tensor_copy(tiles_f[:, :], count_i[:, :]))
            link(dve.tensor_tensor_scan(tile_end[:, :], ones[:, 0:E], tiles_f[:, :], 0.0, ALU.mult, ALU.add))
            link(dve.tensor_tensor(tile_start[:, :], tile_end[:, :], tiles_f[:, :], ALU.subtract))
            link(dve.tensor_scalar(tiles_f[:, :], tile_start[:, :], float(P), None, ALU.mult))
            link(dve.tensor_tensor(work2[:, :, :], running[:, :, :], work[:, :, :], ALU.subtract))
            link(dve.tensor_tensor(work2[:, :, :], work2[:, :, :], ps_prefix.rearrange("p (b e) -> p b e", e=E), ALU.add))
            link(dve.tensor_tensor(work2[:, :, :], work2[:, :, :],
                                   tiles_f[:, :].unsqueeze(1).to_broadcast([S, BATCH, E]), ALU.add))
            for n in range(TOP):
                link(dve.tensor_tensor(work[:, :, :], work2[:, :, :], first[n][:, :, :], ALU.mult))
                link(dve.tensor_reduce(slot_f[:, n, :], work[:, :, :], AX.X, ALU.add))
            link(dve.tensor_copy(rows[:, :, REC_SLOT], slot_f[:, 0, :]))
            dve.tensor_copy(slot_i[:, :, :], slot_f[:, :, :]).then_inc(slots_ready, 1)
            link(dve.tensor_scalar(tile_expert[:, :], tile_no[:, :], tile_start[0:1, 1:2], None, ALU.is_ge))
            for e in range(2, E):
                link(dve.scalar_tensor_tensor(tile_expert[:, :], tile_no[:, :], tile_start[0:1, e:e + 1],
                                              tile_expert[:, :], ALU.is_ge, ALU.add))
            dve.tensor_copy(tile_expert_i[:, :], tile_expert[:, :]).then_inc(tile_expert_ready, 1)

            def body(s, par, active):
                if active(1):
                    t = s - 1
                    x, mine = x_in[1 - par], my_slot[1 - par]
                    dve.wait_ge(x_loaded[1 - par], 16 * (t // 2 + 1) if isinstance(t, int) else (t - (1 - par) + 2) * 8)
                    after(dve, slot_moved, t - 1)
                    after(dve, weight_known, t)
                    after(dve, dest_known, t)
                    dve.tensor_scalar(is_first[:, :], x[:, REC_SLOT:REC_SLOT + 1], mine[:, 0:1], None,
                                      ALU.is_equal).then_inc(first_known, 1)
                    dve.wait_ge(first_known, t + 1)
                    dve.tensor_scalar(second_p[:, :], is_first[:, :], 0.0, x[:, REC_P2:REC_P2 + 1], ALU.is_equal,
                                      ALU.mult).then_inc(second_known, 1)
                    dve.tensor_scalar(pad_row[:, :], x[:, REC_ID:REC_ID + 1], 0.0, trash_row[:, 0:1], ALU.is_equal,
                                      ALU.mult).then_inc(pad_known, 1)
                    dve.tensor_scalar(mine[:, :], mine[:, :], float(2 * P), None, ALU.add).then_inc(slot_moved, 1)
                    dve.wait_ge(second_known, t + 1)
                    dve.scalar_tensor_tensor(weight[1 - par][:, :], is_first[:, :], x[:, REC_P1:REC_P1 + 1],
                                             second_p[:, :], ALU.mult, ALU.add).then_inc(weight_known, 1)
                    dve.wait_ge(pad_known, t + 1)
                    after(dve, y_added, 16 * (t - 1) if isinstance(t, int) else (t - 1) * 16)
                    dve.scalar_tensor_tensor(dest[1 - par][:, :], pad_row[:, :], -1.0, x[:, REC_ID:REC_ID + 1],
                                             ALU.add, ALU.add).then_inc(dest_known, 1)
                if active(2):
                    t = s - 2
                    dve.wait_ge(y_done, t + 1)
                    dve.wait_ge(weight_known, t + 1)
                    after(dve, y_added, 16 * (t - 1) if isinstance(t, int) else (t - 1) * 16)
                    dve.tensor_scalar(y_sb[par][:, :], ps_y[:, 0:D], weight[par][:, 0:1], None,
                                      ALU.mult).then_inc(y_ready, 1)
                if active(1):
                    t = s - 1
                    dve.wait_ge(silu_done, t + 1)
                    after(dve, ht_done, t - 1)
                    dve.tensor_tensor(hidden[1 - par][:, :], gated[:, :], ps_h[1 - par][:, 1, :],
                                      ALU.mult).then_inc(hidden_ready, 1)

            peeled = run_steps(dve, body, HEAD, END, TILES)
            for s in range(END, ALL):
                peeled(s, TILES)

        @block.scalar
        def _(act):
            act.wait_ge(gap_ready, 1)
            act.activation(small[:, :], small[:, :], ACT.Exp).then_inc(gap_exp, 1)

            def body(s, par, active):
                if active(0):
                    act.wait_ge(xt_done, s + 1)
                    after(act, h_done, s - 1)
                    act.activation(x_t[par][:, :, :], ps_xt[:, :, :], ACT.Copy).then_inc(xt_copied, 1)
                if active(2):
                    act.wait_ge(ht_done, s - 1)
                    act.activation(hidden_t[0][:, :, :], ps_ht[:, :, :], ACT.Copy).then_inc(ht_copied, 1)
                if active(1):
                    act.wait_ge(h_done, s)
                    after(act, hidden_ready, s - 1)
                    act.activation(gated[:, :], ps_h[1 - par][:, 0, :], ACT.Silu).then_inc(silu_done, 1)

            peeled = run_steps(act, body, HEAD, END, TILES)
            for s in range(END, ALL):
                peeled(s, TILES)

        @block.tensor
        def _(pe):
            pe.wait_ge(both_ready, 1)
            pe.wait_ge(made, 6)
            choice = both[:, :, :].rearrange("p b e -> p (b e)")
            pe.matmul(ps_prefix, before[:, :], choice, start=True, stop=True)
            pe.matmul(ps_total, ones[:, :], choice, start=True, stop=True).then_inc(prefix_done, 1)
            pe.wait_ge(slots_ready, 1)
            pe.wait_ge(tile_expert_ready, 1)
            pe.wait_ge(weights_in, 16 * 2 * E)

            def body(s, par, active):
                if active(0):
                    pe.wait_ge(x_loaded[par], 16 * (s // 2 + 1) if isinstance(s, int) else (s - par + 2) * 8)
                    after(pe, xt_copied, s)
                    for k in range(DK):
                        mm = pe.transpose(ps_xt[:, k, :], x_in[par][:, k * P:(k + 1) * P], ident[:, :])
                    mm.then_inc(xt_done, 1)
                if active(2):
                    pe.wait_ge(hidden_ready, s - 1)
                    for c in range(HK):
                        mm = pe.transpose(ps_ht[:, c, :], hidden[par][:, c * P:(c + 1) * P], ident[:, :])
                    mm.then_inc(ht_done, 1)
                if active(1):
                    t = s - 1
                    e = expert_of(t)
                    pe.wait_ge(xt_copied, t + 1)
                    after(pe, hidden_ready, t - 1)
                    for half in range(2):
                        for k in range(DK):
                            mm = pe.matmul(ps_h[1 - par][:, half, :], x_t[1 - par][:, k, :],
                                           W12[:, bass.ds(e * (DK * 2 * HID) + (k * 2 + half) * HID, HID)],
                                           start=(k == 0), stop=(k == DK - 1))
                    mm.then_inc(h_done, 1)
                if active(2):
                    t = s - 2
                    e = expert_of(t)
                    pe.wait_ge(ht_copied, t + 1)
                    after(pe, y_ready, t)
                    for c in range(HK):
                        mm = pe.matmul(ps_y[:, 0:D], hidden_t[0][:, c, :],
                                       W3[:, bass.ds(e * (HK * D) + c * D, D)],
                                       start=(c == 0), stop=(c == HK - 1))
                    mm.then_inc(y_done, 1)

            def expert_of(t):
                at = tile_expert_i[0:1, t:t + 1] if isinstance(t, int) else tile_expert_i[0:1, bass.ds(t, 1)]
                return pe.value_load(at, min_val=0, max_val=E - 1)

            peeled = run_steps(pe, body, HEAD, END, TILES)
            for s in range(END, ALL):
                peeled(s, TILES)


def kernel(**inputs):
    import numpy as np
    import concourse.bacc as bacc
    from concourse import mybir as mb
    from concourse.bass_utils import run_bass_kernel_spmd

    a = {k: np.asarray(v) for k, v in inputs.items()}
    side = 16
    grid = 6
    x = a["x"].reshape(BATCH, 3, grid, side, grid, side)
    arrays = {
        "patches": x.transpose(1, 3, 5, 0, 2, 4).reshape(F, IMG_TOKENS),
        "txt": a["txt"].reshape(BATCH * TXT, D),
        "w_lin": a["L0_tok_W_lin"].T,
        "base_rows": np.concatenate([a["L0_tok_class_token"].reshape(1, D),
                                     np.broadcast_to(a["L0_tok_b_lin"][None, :], (IMG, D))], axis=0),
        "pos": a["L0_tok_position_embeddings"].reshape(1 + IMG, D),
        "w_down": np.concatenate([a["L0_attn_W_dq"], a["L0_attn_W_dkv"]], axis=1),
        "gamma": np.concatenate([a["L0_attn_q_ln_g"], a["L0_attn_kv_ln_g"]]).reshape(P, 1),
        "beta": np.concatenate([a["L0_attn_q_ln_b"], a["L0_attn_kv_ln_b"]]).reshape(P, 1),
        "w_uq": a["L0_attn_W_uq"],
        "w_ukv": a["L0_attn_W_ukv"],
        "w_o": a["L0_attn_W_o"].T,
        "w12": a["L0_ffn_w12"].transpose(0, 2, 1),
        "w3": a["L0_ffn_w3"].transpose(0, 2, 1),
        "gate": a["L0_ffn_gate_w"].T,
    }
    arrays = {k: np.ascontiguousarray(v) for k, v in arrays.items()}
    nc = bacc.Bacc("TRN2", target_bir_lowering=False, num_devices=1)
    args = {k: nc.dram_tensor(k, v.shape, mb.dt.from_np(v.dtype), kind="ExternalInput").ap() for k, v in arrays.items()}
    out = nc.dram_tensor("out", [OUT_ROWS, D], mb.dt.float32, kind="ExternalOutput").ap()
    build(nc, out=out, **args)
    r = run_bass_kernel_spmd(nc, [arrays], core_ids=[0])
    return r.results[0]["out"][0:TOKENS].reshape(BATCH, S, D)
```

```python
import concourse.bass as bass
from concourse import mybir
from contextlib import ExitStack

P = 128
BATCH, IMG, TXT = 64, 36, 32
S = 1 + IMG + TXT
TOKENS = BATCH * S
TOKEN_TILES = -(-TOKENS // P)
PADDED = TOKEN_TILES * P
D = 256
F = 768
FK = F // P
DK = D // P
IMG_TOKENS = BATCH * IMG
PER_TILE = P // IMG
EMB = PER_TILE * IMG
IMG_TILES = -(-BATCH // PER_TILE)
HEADS, DH = 16, 16
GROUPS = 4
UNITS = HEADS // GROUPS
PAIR = 2 * S
PROJ = D // 4
E = 8
TOP = 2
HID = 512
HK = HID // P
TILES = (TOKENS * TOP - E) // P + E
SLOTS = TILES * P
REC = D + 4
REC_ID, REC_SLOT, REC_P1, REC_P2 = D, D + 1, D + 2, D + 3
OUT_ROWS = TOKENS + P
EPS = 1e-5
MASKED = -1e30


def build(nc, patches, txt, w_lin, b_lin, cls, pos, w_down, gamma, beta, w_uq, w_ukv, w_o, w12, w3, gate, out):
    fp32 = mybir.dt.float32
    i32 = mybir.dt.int32
    ALU = mybir.AluOpType
    ACT = mybir.ActivationFunctionType
    AX = mybir.AxisListType

    h_rows = nc.dram_tensor("h_rows", [PADDED, D], fp32, kind="Internal").ap()
    slot_rows = nc.dram_tensor("slot_rows", [SLOTS, REC], fp32, kind="Internal").ap()

    ctx = ExitStack()
    with ctx:
        sems = {}

        def sem(name):
            sems[name] = ctx.enter_context(nc.semaphore(name))
            return sems[name]

        def sb(stack, name, shape, dt=fp32):
            return stack.enter_context(nc.sbuf_tensor(name, shape, dt))

        def ps(stack, name, shape, dt=fp32):
            return stack.enter_context(nc.psum_tensor(name, shape, dt))

        rows = sb(ctx, "rows", [P, TOKEN_TILES, REC])
        scores_all = sb(ctx, "scores_all", [P, TOKEN_TILES, E])
        ident = sb(ctx, "ident", [P, P])
        consts_ready = sem("consts_ready")
        pads_cleared = sem("pads_cleared")

        until_gate(nc, sb, ps, sem, locals())
        route_and_experts(nc, ctx, sb, ps, sem, locals())


def until_gate(nc, sb, ps, sem, env):
    with ExitStack() as ctx:
        w_down_sb = sb(ctx, "w_down_sb", [P, DK, P])
        gamma_sb = sb(ctx, "gamma_sb", [P, 1])
        beta_sb = sb(ctx, "beta_sb", [P, 1])
        w_qk = [sb(ctx, f"w_qk{n}", [P, UNITS, P]) for n in range(2)]
        w_v = sb(ctx, "w_v", [P, D])
        w_o_sb = sb(ctx, "w_o_sb", [P, DK, D])
        gate_sb = sb(ctx, "gate_sb", [P, DK, E])
        minus_half = sb(ctx, "minus_half", [P, 2])
        c_t = sb(ctx, "c_t", [P, PADDED])
        o_t = sb(ctx, "o_t", [P, DK, PADDED])
        k_diag = sb(ctx, "k_diag", [P, UNITS, GROUPS, PAIR])
        v_sb = [sb(ctx, f"v_sb{n}", [S, HEADS, DH + 1]) for n in range(2)]
        env = {**env, **locals()}
        embed(nc, sb, ps, sem, env)
        compress(nc, sb, ps, sem, env)
        attention(nc, sb, ps, sem, env)
        output(nc, sb, ps, sem, env)


def after(eng, semaphore, value):
    if not (isinstance(value, int) and value <= 0):
        eng.wait_ge(semaphore, value)


def run_steps(eng, body, head, end, total):
    def peeled(n, count):
        body(n, n % 2, lambda k: 0 <= n - k < count)

    for n in range(head):
        peeled(n, total)
    with eng.Fori(0, (end - head) // 2) as i:
        for j in range(2):
            body(i * 2 + (head + j), (head + j) % 2, lambda k: True)
    return peeled


def parity_count(unit, s, par):
    return 16 * unit * (s // 2 + 1) if isinstance(s, int) else (s - par + 2) * (8 * unit)


def row_of(rows, t):
    if isinstance(t, int):
        return rows[:, t, 0:D]
    return rows[:, bass.ds(t, 1), 0:D].rearrange("p a d -> p (a d)")


def embed(nc, sb, ps, sem, env):
    ALU = env["ALU"]
    patches, txt, h_rows, slot_rows, ident = (env[n] for n in ("patches", "txt", "h_rows", "slot_rows", "ident"))
    w_down_sb, gamma_sb, beta_sb, w_qk, w_v, w_o_sb, gate_sb, minus_half, o_t, k_diag, v_sb = (
        env[n] for n in ("w_down_sb", "gamma_sb", "beta_sb", "w_qk", "w_v", "w_o_sb", "gate_sb", "minus_half",
                         "o_t", "k_diag", "v_sb"))
    out, consts_ready, pads_cleared = env["out"], env["consts_ready"], env["pads_cleared"]
    by_batch = h_rows[0:TOKENS, :].rearrange("(b s) d -> b s d", s=S)
    with ExitStack() as ctx:
        w_lin_sb = sb(ctx, "w_lin_sb", [P, FK, D])
        patch_sb = [sb(ctx, f"patch_sb{n}", [P, FK, EMB]) for n in range(2)]
        emb_sb = [sb(ctx, f"emb_sb{n}", [EMB, D]) for n in range(2)]
        base_sb = sb(ctx, "base_sb", [EMB, D])
        img_pos_sb = sb(ctx, "img_pos_sb", [EMB, D])
        cls_sb = sb(ctx, "cls_sb", [BATCH, D])
        cls_pos_sb = sb(ctx, "cls_pos_sb", [BATCH, D])
        zero_rows = sb(ctx, "zero_rows", [P, REC])
        ps_emb = [ps(ctx, f"ps_emb{n}", [P, 512])[0:EMB, 0:D] for n in range(2)]
        patch_in = [sem(f"patch_in{n}") for n in range(2)]
        w_lin_in, small_in, base_in = sem("w_lin_in"), sem("small_in"), sem("base_in")
        emb_mm, emb_added = sem("emb_mm"), sem("emb_added")
        emb_stored = [sem(f"emb_stored{n}") for n in range(2)]
        base_ready, rows_laid, zeros_made = sem("base_ready"), sem("rows_laid"), sem("zeros_made")
        SMALL = 8
        block = ctx.enter_context(nc.Block())

        def batches(t):
            return min(PER_TILE, BATCH - t * PER_TILE)

        @block.sync
        def _(sp):
            sp.dma_start(w_lin_sb[:, :, :], env["w_lin"].rearrange("(k p) d -> p k d", p=P)).then_inc(w_lin_in, 16)
            for t in range(IMG_TILES):
                n = batches(t) * IMG
                if t >= 2:
                    sp.wait_ge(emb_mm, t - 1)
                sp.dma_start(patch_sb[t % 2][:, :, 0:n],
                             patches[:, t * EMB:t * EMB + n].rearrange("(k p) n -> p k n", p=P)
                             ).then_inc(patch_in[t % 2], 16)
                if t == 1:
                    sp.dma_start(w_down_sb[:, :, :],
                                 env["w_down"].rearrange("(k p) d -> p k d", p=P)).then_inc(small_in, 16)
                    sp.dma_start(gamma_sb[:, :], env["gamma"]).then_inc(small_in, 16)
                    sp.dma_start(beta_sb[:, :], env["beta"]).then_inc(small_in, 16)
                    sp.wait_ge(zeros_made, 3)
                    spread = [w[:, :, :].rearrange("p u (g d) -> p (u g) d", g=GROUPS) for w in w_qk]
                    sp.dma_start(spread[0][0:PROJ, :, 0:DH],
                                 env["w_uq"].rearrange("p (h d) -> p h d", d=DH)).then_inc(small_in, 16)
                    sp.dma_start(spread[1][PROJ:P, :, 0:DH],
                                 env["w_ukv"][:, 0:D].rearrange("p (h d) -> p h d", d=DH)).then_inc(small_in, 16)
                    sp.dma_start(w_v[PROJ:P, :], env["w_ukv"][:, D:2 * D]).then_inc(small_in, 16)
                    sp.dma_start(w_o_sb[:, :, :],
                                 env["w_o"].rearrange("(k p) d -> p k d", p=P)).then_inc(small_in, 16)
                    sp.dma_start(gate_sb[:, :, :],
                                 env["gate"].rearrange("(k p) e -> p k e", p=P)).then_inc(small_in, 16)
            sp.wait_ge(small_in, 16 * SMALL)

        @block.gpsimd
        def _(pool):
            for w in w_qk:
                pool.memset(w[:, :, :], 0.0).then_inc(zeros_made, 1)
            pool.memset(w_v[0:PROJ, :], 0.0).then_inc(zeros_made, 1)
            pool.memset(zero_rows[:, :], 0.0).then_inc(zeros_made, 1)
            pool.memset(minus_half[:, :], -0.5).then_inc(consts_ready, 1)
            for n in range(2):
                pool.memset(v_sb[n][:, :, :], 1.0).then_inc(consts_ready, 1)
            pool.memset(k_diag[:, :, :, :], 0.0).then_inc(consts_ready, 1)
            pool.memset(o_t[:, :, TOKENS:PADDED], 0.0).then_inc(consts_ready, 1)
            pool.memset(ident[:, :], 0.0).then_inc(consts_ready, 1)
            pool.wait_ge(consts_ready, 6)
            pool.affine_select(out=ident[:, :], in_=ident[:, :], compare_op=ALU.not_equal, fill=1.0, base=0,
                               pattern=[[-1, P]], channel_multiplier=1).then_inc(consts_ready, 1)
            pool.wait_ge(zeros_made, 4)
            for t in range(0, TILES, 4):
                pool.dma_start(slot_rows[t * P:(t + 4) * P, :].rearrange("(n p) c -> p n c", p=P),
                               zero_rows[:, :].unsqueeze(1).to_broadcast([P, 4, REC])).then_inc(pads_cleared, 16)
            pool.dma_start(out[PADDED:OUT_ROWS, :], zero_rows[0:OUT_ROWS - PADDED, 0:D]).then_inc(pads_cleared, 16)
            pool.dma_start(h_rows[TOKENS:PADDED, :], zero_rows[0:PADDED - TOKENS, 0:D]).then_inc(pads_cleared, 16)
            pool.wait_ge(pads_cleared, 16 * (TILES // 4 + 2))

        @block.scalar
        def _(act):
            act.dma_start(base_sb[:, :], env["b_lin"].to_broadcast([EMB, D])).then_inc(base_in, 16)
            for n in range(PER_TILE):
                act.dma_start(img_pos_sb[n * IMG:(n + 1) * IMG, :], env["pos"][1:1 + IMG, :]).then_inc(base_in, 16)
            act.dma_start(cls_sb[:, :], env["cls"].to_broadcast([BATCH, D])).then_inc(base_in, 16)
            act.dma_start(cls_pos_sb[:, :], env["pos"][0:1, :].to_broadcast([BATCH, D])).then_inc(base_in, 16)
            act.dma_start(by_batch[:, 1 + IMG:S, :], txt.rearrange("(b t) d -> b t d", t=TXT)).then_inc(rows_laid, 16)
            act.wait_ge(base_ready, 2)
            act.dma_start(by_batch[:, 0, :], cls_sb[:, :]).then_inc(rows_laid, 16)
            for t in range(IMG_TILES):
                act.wait_ge(emb_added, t + 1)
                for n in range(batches(t)):
                    act.dma_start(by_batch[t * PER_TILE + n, 1:1 + IMG, :],
                                  emb_sb[t % 2][n * IMG:(n + 1) * IMG, :]).then_inc(emb_stored[t % 2], 16)
            act.wait_ge(rows_laid, 32)
            for n in range(2):
                act.wait_ge(emb_stored[n], 16 * sum(batches(t) for t in range(n, IMG_TILES, 2)))

        @block.vector
        def _(dve):
            dve.wait_ge(base_in, 16 * (PER_TILE + 3))
            dve.tensor_tensor(base_sb[:, :], base_sb[:, :], img_pos_sb[:, :], ALU.add).then_inc(base_ready, 1)
            dve.tensor_tensor(cls_sb[:, :], cls_sb[:, :], cls_pos_sb[:, :], ALU.add).then_inc(base_ready, 1)
            dve.wait_ge(base_ready, 2)
            for t in range(IMG_TILES):
                n = batches(t) * IMG
                dve.wait_ge(emb_mm, t + 1)
                if t >= 2:
                    dve.wait_ge(emb_stored[t % 2], 16 * PER_TILE * (t // 2))
                dve.tensor_tensor(emb_sb[t % 2][0:n, :], ps_emb[t % 2][0:n, :], base_sb[0:n, :],
                                  ALU.add).then_inc(emb_added, 1)

        @block.tensor
        def _(pe):
            pe.wait_ge(w_lin_in, 16)
            for t in range(IMG_TILES):
                n = batches(t) * IMG
                pe.wait_ge(patch_in[t % 2], 16 * (t // 2 + 1))
                if t >= 2:
                    pe.wait_ge(emb_added, t - 1)
                for k in range(FK):
                    mm = pe.matmul(ps_emb[t % 2][0:n, :], patch_sb[t % 2][:, k, 0:n], w_lin_sb[:, k, :],
                                   start=(k == 0), stop=(k == FK - 1))
                mm.then_inc(emb_mm, 1)


def compress(nc, sb, ps, sem, env):
    ALU, ACT = env["ALU"], env["ACT"]
    h_rows, rows, ident, minus_half, w_down_sb, gamma_sb, beta_sb, c_t = (
        env[n] for n in ("h_rows", "rows", "ident", "minus_half", "w_down_sb", "gamma_sb", "beta_sb", "c_t"))
    with ExitStack() as ctx:
        stats1 = sb(ctx, "stats1", [P, 6])
        mv1 = sb(ctx, "mv1", [P, 2])
        rstd1 = sb(ctx, "rstd1", [P, 1])
        h_in = [sb(ctx, f"h_in{n}", [P, D]) for n in range(2)]
        xn = [sb(ctx, f"xn{n}", [P, D]) for n in range(2)]
        xn_t = [sb(ctx, f"xn_t{n}", [P, DK, P]) for n in range(2)]
        stats_c = sb(ctx, "stats_c", [P, 2, 6])
        mv_c = sb(ctx, "mv_c", [P, 2, 2])
        rstd_c = sb(ctx, "rstd_c", [P, 2])
        cn = [sb(ctx, f"cn{n}", [P, P]) for n in range(2)]
        ps_xt = [ps(ctx, f"ps_xt{n}", [P, 512])[:, 0:D].rearrange("p (k s) -> p k s", k=DK) for n in range(2)]
        ps_down = [ps(ctx, f"ps_down{n}", [P, 512])[:, 0:P] for n in range(2)]
        ps_ct = [ps(ctx, f"ps_ct{n}", [P, 512])[:, 0:P] for n in range(2)]
        loaded = [sem(f"loaded{n}") for n in range(2)]
        h_kept = sem("h_kept")
        stats1_done, aggr1, mv1_done, rstd1_done, xn_ready = (
            sem("stats1_done"), sem("aggr1"), sem("mv1_done"), sem("rstd1_done"), sem("xn_ready"))
        xt_done, xt_copied, down_done = sem("xt_done"), sem("xt_copied"), sem("down_done")
        stats_c_done, aggr_c, mv_c_done, rstd_c_done, cn_ready = (
            sem("stats_c_done"), sem("aggr_c"), sem("mv_c_done"), sem("rstd_c_done"), sem("cn_ready"))
        ct_done, ct_copied = sem("ct_done"), sem("ct_copied")
        N = TOKEN_TILES
        HEAD, ALL = 5, N + 3
        END = HEAD + (N - HEAD) // 2 * 2
        block = ctx.enter_context(nc.Block())

        def run(eng, body):
            peeled = run_steps(eng, body, HEAD, END, N)
            for s in range(END, ALL):
                peeled(s, N)

        @block.sync
        def _(sp):
            def body(s, par, active):
                if active(0):
                    after(sp, xn_ready, s - 1)
                    after(sp, h_kept, s - 1)
                    src = h_rows[s * P:(s + 1) * P, :] if isinstance(s, int) else h_rows[bass.ds(s * P, P), :]
                    sp.dma_start(h_in[par][:, :], src).then_inc(loaded[par], 16)
            run(sp, body)

        @block.gpsimd
        def _(pool):
            def body(s, par, active):
                if active(0):
                    pool.wait_ge(mv1_done, s + 1)
                    after(pool, xn_ready, s)
                    pool.tensor_tensor(rstd1[:, :], mv1[:, 1:2], minus_half[:, 0:1], ALU.pow).then_inc(rstd1_done, 1)
                if active(2):
                    pool.wait_ge(mv_c_done, s - 1)
                    after(pool, cn_ready, s - 2)
                    pool.tensor_tensor(rstd_c[:, :], mv_c[:, :, 1], minus_half[:, :], ALU.pow).then_inc(rstd_c_done, 1)
                if active(0):
                    pool.wait_ge(rstd1_done, s + 1)
                    pool.tensor_copy(row_of(rows, s), h_in[par][:, :]).then_inc(h_kept, 1)
            run(pool, body)

        @block.scalar
        def _(act):
            def body(s, par, active):
                if active(3):
                    act.wait_ge(ct_done, s - 2)
                    b = s - 3
                    dst = c_t[:, b * P:(b + 1) * P] if isinstance(b, int) else c_t[:, bass.ds(b * P, P)]
                    act.activation(dst, ps_ct[1 - par], ACT.Identity, bias=beta_sb[:, 0:1],
                                   scale=gamma_sb[:, 0:1]).then_inc(ct_copied, 1)
                if active(1):
                    act.wait_ge(xt_done, s)
                    after(act, down_done, s - 2)
                    act.activation(xn_t[1 - par][:, :, :], ps_xt[1 - par], ACT.Copy).then_inc(xt_copied, 1)
            run(act, body)

        @block.tensor
        def _(pe):
            def body(s, par, active):
                if active(2):
                    pe.wait_ge(xt_copied, s - 1)
                    after(pe, cn_ready, s - 3)
                    for k in range(DK):
                        mm = pe.matmul(ps_down[par], xn_t[par][:, k, :], w_down_sb[:, k, :], start=(k == 0),
                                       stop=(k == DK - 1))
                    mm.then_inc(down_done, 1)
                if active(3):
                    pe.wait_ge(cn_ready, s - 2)
                    after(pe, ct_copied, s - 4)
                    pe.transpose(ps_ct[1 - par], cn[1 - par][:, :], ident[:, :]).then_inc(ct_done, 1)
                if active(1):
                    pe.wait_ge(xn_ready, s)
                    after(pe, xt_copied, s - 2)
                    for k in range(DK):
                        mm = pe.transpose(ps_xt[1 - par][:, k, :], xn[1 - par][:, k * P:(k + 1) * P], ident[:, :])
                    mm.then_inc(xt_done, 1)
            run(pe, body)

        @block.vector
        def _(dve):
            def body(s, par, active):
                if active(1):
                    dve.wait_ge(rstd1_done, s)
                    after(dve, xt_done, s - 2)
                    dve.tensor_scalar(xn[1 - par][:, :], h_in[1 - par][:, :], mv1[:, 0:1], rstd1[:, 0:1], ALU.subtract,
                                      ALU.mult).then_inc(xn_ready, 1)
                if active(3):
                    dve.wait_ge(rstd_c_done, s - 2)
                    after(dve, ct_done, s - 4)
                    for n in range(2):
                        last = dve.tensor_scalar(cn[1 - par][:, n * PROJ:(n + 1) * PROJ],
                                                 ps_down[1 - par][:, n * PROJ:(n + 1) * PROJ], mv_c[:, n, 0:1],
                                                 rstd_c[:, n:n + 1], ALU.subtract, ALU.mult)
                    last.then_inc(cn_ready, 1)
                if active(0):
                    dve.wait_ge(loaded[par], parity_count(1, s, par))
                    dve.bn_stats(stats1[:, :], h_in[par][:, :]).then_inc(stats1_done, 1)
                if active(2):
                    dve.wait_ge(down_done, s - 1)
                    dve.bn_stats(stats_c[:, 0, :], ps_down[par][:, 0:PROJ])
                if active(0):
                    dve.wait_ge(stats1_done, s + 1)
                if active(2):
                    dve.bn_stats(stats_c[:, 1, :], ps_down[par][:, PROJ:P]).then_inc(stats_c_done, 1)
                if active(0):
                    dve.bn_aggr(mv1[:, :], stats1[:, :]).then_inc(aggr1, 1)
                    dve.wait_ge(aggr1, s + 1)
                if active(2):
                    dve.wait_ge(stats_c_done, s - 1)
                if active(0):
                    dve.tensor_scalar(mv1[:, 1:2], mv1[:, 1:2], EPS, None, ALU.add).then_inc(mv1_done, 1)
                if active(2):
                    for n in range(2):
                        stat = dve.bn_aggr(mv_c[:, n, :], stats_c[:, n, :])
                    stat.then_inc(aggr_c, 1)
                    dve.wait_ge(aggr_c, s - 1)
                    dve.tensor_scalar(mv_c[:, :, 1], mv_c[:, :, 1], EPS, None, ALU.add).then_inc(mv_c_done, 1)
            run(dve, body)


def attention(nc, sb, ps, sem, env):
    ALU, ACT, AX = env["ALU"], env["ACT"], env["AX"]
    w_qk, w_v, c_t, o_t, k_diag, v_sb, ident = (
        env[n] for n in ("w_qk", "w_v", "c_t", "o_t", "k_diag", "v_sb", "ident"))
    with ExitStack() as ctx:
        c_pair = sb(ctx, "c_pair", [P, PAIR])
        q_t = sb(ctx, "q_t", [P, UNITS, PAIR])
        scores = [sb(ctx, f"scores{n}", [S, HEADS, S]) for n in range(2)]
        probs = [sb(ctx, f"probs{n}", [S, HEADS, S]) for n in range(2)]
        zeros_out = sb(ctx, "zeros_out", [S, HEADS, S])
        row_max = sb(ctx, "row_max", [S, HEADS])
        p_t = [sb(ctx, f"p_t{n}", [S, GROUPS * S]) for n in range(2)]
        inv_sum = sb(ctx, "inv_sum", [S, HEADS])
        o_norm = sb(ctx, "o_norm", [S, HEADS, DH])
        ps_scores = ps(ctx, "ps_scores", [P, UNITS, 512])
        ps_pt = [ps(ctx, f"ps_pt{n}", [P, 512]) for n in range(2)]
        ps_out = ps(ctx, "ps_out", [P, 512])
        ps_v = ps(ctx, "ps_v", [P, 512])[0:S, 0:D]
        ps_o = ps_out[0:S, 0:HEADS * (DH + 1)].rearrange("p (h d) -> p h d", h=HEADS)
        ps_ot = ps_out[:, HEADS * (DH + 1):HEADS * (DH + 1) + DK * S].rearrange("p (k s) -> p k s", k=DK)

        pair_ready = sem("pair_ready")
        k_copied = sem("k_copied")
        qk_done, q_copied = sem("qk_done"), sem("q_copied")
        v_done, v_copied = sem("v_done"), sem("v_copied")
        scores_done, scores_copied, causal_done = sem("scores_done"), sem("scores_copied"), sem("causal_done")
        zero_marked, zero_masked, max_done, shifted, exp_done = (
            sem("zero_marked"), sem("zero_masked"), sem("max_done"), sem("shifted"), sem("exp_done"))
        pt_done, pt_copied, pv_unit = sem("pt_done"), sem("pt_copied"), sem("pv_unit")
        inv_done, o_ready, ot_done, ot_copied = sem("inv_done"), sem("o_ready"), sem("ot_done"), sem("ot_copied")
        HEAD, END, ALL = 6, BATCH, BATCH + 4
        block = ctx.enter_context(nc.Block())

        def run(eng, body):
            peeled = run_steps(eng, body, HEAD, END, BATCH)
            for s in range(END, ALL):
                peeled(s, BATCH)

        @block.gpsimd
        def _(pool):
            masked = pool.to_reg(MASKED)

            def body(s, par, active):
                if active(0) and par == 0:
                    after(pool, v_done, s)
                    src = c_t[:, s * S:s * S + PAIR] if isinstance(s, int) else c_t[:, bass.ds(s * S, PAIR)]
                    pool.tensor_copy(c_pair[:, :], src).then_inc(pair_ready, 2)
                if active(1):
                    copied = s if isinstance(s, int) else pool.to_reg(s)

                    pool.wait_ge(env["consts_ready"], 7)
                    pool.wait_ge(scores_copied, copied)
                    sc = scores[1 - par]
                    pool.affine_select(out=sc[:, :, :], in_=sc[:, :, :], compare_op=ALU.is_ge, fill=masked, base=0,
                                       pattern=[[0, HEADS], [-1, S]], channel_multiplier=1).then_inc(causal_done, 1)

            run(pool, body)

        def key_block(eng_copy, g):
            part = slice(32 * g, 32 * g + 32)
            return eng_copy(k_diag[part, :, g, :].rearrange("p (a u) s -> p a u s", a=2),
                            ps_scores[part, 2:4, 0:2 * PAIR].rearrange("p a (u s) -> p a u s", u=2))

        ON_ACT = 2

        @block.scalar
        def _(act):
            def body(s, par, active):
                def copy_turned(u):
                    n = (s - 3) * UNITS + u
                    act.wait_ge(pt_done, n + 1)
                    after(act, pv_unit, n - 1)
                    act.activation(p_t[u % 2][:, :], ps_pt[u % 2][0:S, 0:GROUPS * S], ACT.Copy).then_inc(pt_copied, 1)

                if active(3):
                    copy_turned(0)
                    copy_turned(1)
                if active(4):
                    b = s - 4
                    act.wait_ge(ot_done, s - 3)
                    dst = o_t[:, :, b * S:(b + 1) * S] if isinstance(b, int) else o_t[:, :, bass.ds(b * S, S)]
                    act.activation(dst, ps_ot, ACT.Copy).then_inc(ot_copied, 1)
                if active(1):
                    act.wait_ge(scores_done, s * UNITS)
                    after(act, shifted, s - 2)
                    act.activation(scores[1 - par][:, :, :].rearrange("p (u g) s -> p u (g s)", u=UNITS),
                                   ps_scores[0:S, :, 0:GROUPS * S], ACT.Copy).then_inc(scores_copied, 1)
                if active(3):
                    copy_turned(2)
                if active(0) and par == 0:
                    act.wait_ge(qk_done, s + 1)
                    for g in range(ON_ACT):
                        key_block(lambda o, i: act.activation(o, i, ACT.Copy), g).then_inc(k_copied, 1)
                if active(3):
                    copy_turned(3)
                if active(0) and par == 0:
                    act.wait_ge(qk_done, s + 2)
                    act.activation(q_t[:, :, :].rearrange("p (a u) s -> p a (u s)", a=2), ps_scores[:, 0:2, 0:2 * PAIR],
                                   ACT.Copy).then_inc(q_copied, 2)
                if active(2):
                    act.wait_ge(shifted, s - 1)
                    act.activation(probs[par][:, :, :], probs[par][:, :, :], ACT.Exp,
                                   scale=float(DH) ** -0.5).then_inc(exp_done, 1)
                if active(1):
                    act.wait_ge(v_done, s)
                    after(act, pv_unit, (s - 2) * UNITS)
                    act.activation(v_sb[1 - par][:, :, 0:DH], ps_v.rearrange("p (h d) -> p h d", h=HEADS),
                                   ACT.Copy).then_inc(v_copied, 1)
            run(act, body)

        @block.tensor
        def _(pe):
            def body(s, par, active):
                at = (1 - par) * S

                def score(u):
                    if u == 0:
                        pe.wait_ge(q_copied, s + par)
                        pe.wait_ge(k_copied, (s + par) * 2)
                        after(pe, scores_copied, s - 1)
                    pe.matmul(ps_scores[0:S, u, 0:GROUPS * S], q_t[:, u, at:at + S], k_diag[:, u, :, at:at + S],
                              start=True, stop=True).then_inc(scores_done, 1)

                def values():
                    after(pe, v_copied, s - 1)
                    pe.matmul(ps_v, c_pair[:, at:at + S], w_v[:, :], start=True, stop=True).then_inc(v_done, 1)

                def turn_output():
                    pe.wait_ge(o_ready, s - 3)
                    for k in range(DK):
                        mm = pe.transpose(ps_ot[:, k, :],
                                          o_norm[:, k * (P // DH):(k + 1) * (P // DH), :].rearrange("p h d -> p (h d)"),
                                          ident[0:S, 0:S])
                    mm.then_inc(ot_done, 1)

                def turn(u):
                    n = (s - 3) * UNITS + u
                    if u == 0:
                        pe.wait_ge(exp_done, s - 2)
                    after(pe, pt_copied, n - 1)
                    for g in range(GROUPS):
                        mm = pe.transpose(ps_pt[u % 2][0:S, g * S:(g + 1) * S], probs[1 - par][:, u * GROUPS + g, :],
                                          ident[0:S, 0:S])
                    mm.then_inc(pt_done, 1)

                def times_v(u):
                    n = (s - 3) * UNITS + u
                    if u == 0:
                        pe.wait_ge(v_copied, s - 2)
                        after(pe, o_ready, s - 3)
                        after(pe, ot_copied, s - 3)
                    pe.wait_ge(pt_copied, n + 1)
                    for g in range(GROUPS):
                        mm = pe.matmul(ps_o[:, u * GROUPS + g, :], p_t[u % 2][:, g * S:(g + 1) * S],
                                       v_sb[1 - par][:, u * GROUPS + g, :], start=True, stop=True)
                    mm.then_inc(pv_unit, 1)

                def project(n):
                    if n == 1:
                        pe.wait_ge(pair_ready, s + 2)
                        after(pe, scores_copied, s)
                    for u in range(UNITS):
                        mm = pe.matmul(ps_scores[:, 2 * n + u // 2, (u % 2) * PAIR:(u % 2 + 1) * PAIR],
                                       w_qk[n][:, u, :], c_pair[:, :], start=True, stop=True)
                    mm.then_inc(qk_done, 1)

                if active(1):
                    score(0)
                if active(3):
                    turn(0)
                if active(1):
                    score(1)
                if active(3):
                    turn(1)
                if active(4):
                    turn_output()
                if active(1):
                    score(2)
                    values()
                    score(3)
                if active(3):
                    times_v(0)
                    turn(2)
                if active(0) and par == 0:
                    project(1)
                if active(3):
                    times_v(1)
                    turn(3)
                if active(0) and par == 0:
                    project(0)
                if active(3):
                    times_v(2)
                    times_v(3)
            run(pe, body)

        @block.vector
        def _(dve):
            def body(s, par, active):
                if active(4):
                    dve.wait_ge(pv_unit, (s - 3) * UNITS)
                    dve.reciprocal(inv_sum[:, :], ps_o[:, :, DH]).then_inc(inv_done, 1)
                    dve.wait_ge(inv_done, s - 3)
                    after(dve, ot_done, s - 4)
                    dve.tensor_tensor(o_norm[:, :, :], ps_o[:, :, 0:DH],
                                      inv_sum[:, :].unsqueeze(2).to_broadcast([S, HEADS, DH]),
                                      ALU.mult).then_inc(o_ready, 1)
                if active(2):
                    dve.wait_ge(causal_done, s - 1)
                    dve.tensor_scalar(zeros_out[:, :, :], scores[par][:, :, :], 0.0, MASKED, ALU.is_equal,
                                      ALU.mult).then_inc(zero_marked, 1)
                    dve.wait_ge(zero_marked, s - 1)
                    dve.tensor_tensor(scores[par][:, :, :], scores[par][:, :, :], zeros_out[:, :, :],
                                      ALU.add).then_inc(zero_masked, 1)
                    dve.wait_ge(zero_masked, s - 1)
                    dve.tensor_reduce(row_max[:, :], scores[par][:, :, :], AX.X, ALU.max).then_inc(max_done, 1)
                    dve.wait_ge(max_done, s - 1)
                    after(dve, pt_done, (s - 3) * UNITS)
                    dve.tensor_tensor(probs[par][:, :, :], scores[par][:, :, :],
                                      row_max[:, :].unsqueeze(2).to_broadcast([S, HEADS, S]),
                                      ALU.subtract).then_inc(shifted, 1)
                if active(0) and par == 0:
                    dve.wait_ge(qk_done, s + 1)
                    for g in range(ON_ACT, GROUPS):
                        key_block(dve.tensor_copy, g).then_inc(k_copied, 1)
            run(dve, body)


def output(nc, sb, ps, sem, env):
    ALU, ACT = env["ALU"], env["ACT"]
    out, rows, scores_all, ident, minus_half, w_o_sb, gate_sb, o_t = (
        env[n] for n in ("out", "rows", "scores_all", "ident", "minus_half", "w_o_sb", "gate_sb", "o_t"))
    with ExitStack() as ctx:
        o_tile = [sb(ctx, f"o_tile{n}", [P, DK, P]) for n in range(2)]
        h_out = [sb(ctx, f"h_out{n}", [P, D]) for n in range(2)]
        stats2 = sb(ctx, "stats2", [P, 6])
        mv2 = sb(ctx, "mv2", [P, 2])
        rstd2 = sb(ctx, "rstd2", [P, 1])
        xn2 = [sb(ctx, f"xn2{n}", [P, D]) for n in range(2)]
        xn2_t = [sb(ctx, f"xn2_t{n}", [P, DK, P]) for n in range(2)]
        ps_wo = [ps(ctx, f"ps_wo{n}", [P, 512])[:, 0:D] for n in range(2)]
        ps_x2t = [ps(ctx, f"ps_x2t{n}", [P, 512])[:, 0:D].rearrange("p (k s) -> p k s", k=DK) for n in range(2)]
        ps_gate = [ps(ctx, f"ps_gate{n}", [P, 512])[:, 0:E] for n in range(2)]
        o_ready, wo_done, h_out_ready = sem("o_tile_ready"), sem("wo_done"), sem("h_out_ready")
        h_stored = [sem(f"h_stored{n}") for n in range(2)]
        stats2_done, aggr2, mv2_done, rstd2_done = (
            sem("stats2_done"), sem("aggr2"), sem("mv2_done"), sem("rstd2_done"))
        xn2_ready, row_kept = sem("xn2_ready"), sem("row_kept")
        x2t_done, x2t_copied, gate_done, gate_copied = (
            sem("x2t_done"), sem("x2t_copied"), sem("gate_done"), sem("gate_copied"))
        N = TOKEN_TILES
        HEAD, ALL = 5, N + 3
        END = HEAD + (N - HEAD) // 2 * 2
        block = ctx.enter_context(nc.Block())

        def run(eng, body):
            peeled = run_steps(eng, body, HEAD, END, N)
            for s in range(END, ALL):
                peeled(s, N)

        @block.sync
        def _(sp):
            def body(s, par, active):
                if active(1):
                    sp.wait_ge(h_out_ready, s)
                    b = s - 1
                    dst = out[b * P:(b + 1) * P, :] if isinstance(b, int) else out[bass.ds(b * P, P), :]
                    sp.dma_start(dst, h_out[1 - par][:, :]).then_inc(h_stored[1 - par], 16)
            run(sp, body)
            for n in range(2):
                sp.wait_ge(h_stored[n], 16 * len(range(n, N, 2)))

        @block.gpsimd
        def _(pool):
            def body(s, par, active):
                if active(1):
                    pool.wait_ge(mv2_done, s)
                    after(pool, xn2_ready, s - 1)
                    pool.tensor_tensor(rstd2[:, :], mv2[:, 1:2], minus_half[:, 0:1], ALU.pow).then_inc(rstd2_done, 1)
                if active(2):
                    pool.wait_ge(xn2_ready, s - 1)
                    pool.tensor_copy(row_of(rows, s - 2), xn2[par][:, :]).then_inc(row_kept, 1)
            run(pool, body)

        @block.scalar
        def _(act):
            def body(s, par, active):
                if active(0):
                    after(act, wo_done, s - 1)
                    src = o_t[:, :, s * P:(s + 1) * P] if isinstance(s, int) else o_t[:, :, bass.ds(s * P, P)]
                    act.activation(o_tile[par][:, :, :], src, ACT.Copy).then_inc(o_ready, 1)
                if active(3):
                    act.wait_ge(x2t_done, s - 2)
                    after(act, gate_done, s - 4)
                    act.activation(xn2_t[1 - par][:, :, :], ps_x2t[1 - par], ACT.Copy).then_inc(x2t_copied, 1)
            run(act, body)

        @block.tensor
        def _(pe):
            def body(s, par, active):
                if active(0):
                    pe.wait_ge(o_ready, s + 1)
                    after(pe, h_out_ready, s - 1)
                    for k in range(DK):
                        mm = pe.matmul(ps_wo[par], o_tile[par][:, k, :], w_o_sb[:, k, :], start=(k == 0),
                                       stop=(k == DK - 1))
                    mm.then_inc(wo_done, 1)
                if active(2):
                    pe.wait_ge(xn2_ready, s - 1)
                    after(pe, x2t_copied, s - 3)
                    for k in range(DK):
                        mm = pe.transpose(ps_x2t[par][:, k, :], xn2[par][:, k * P:(k + 1) * P], ident[:, :])
                    mm.then_inc(x2t_done, 1)
                if active(3):
                    pe.wait_ge(x2t_copied, s - 2)
                    after(pe, gate_copied, s - 4)
                    for k in range(DK):
                        mm = pe.matmul(ps_gate[1 - par], xn2_t[1 - par][:, k, :], gate_sb[:, k, :], start=(k == 0),
                                       stop=(k == DK - 1))
                    mm.then_inc(gate_done, 1)
            run(pe, body)

        @block.vector
        def _(dve):
            def body(s, par, active):
                if active(1):
                    b = s - 1
                    dve.wait_ge(wo_done, s)
                    after(dve, h_stored[1 - par], 16 * (b // 2) if isinstance(b, int) else (b - (1 - par)) * 8)
                    dve.tensor_tensor(h_out[1 - par][:, :], ps_wo[1 - par], row_of(rows, b),
                                      ALU.add).then_inc(h_out_ready, 1)
                if active(2):
                    dve.wait_ge(rstd2_done, s - 1)
                    after(dve, x2t_done, s - 3)
                    after(dve, row_kept, s - 3)
                    dve.tensor_scalar(xn2[par][:, :], h_out[par][:, :], mv2[:, 0:1], rstd2[:, 0:1], ALU.subtract,
                                      ALU.mult).then_inc(xn2_ready, 1)
                if active(1):
                    dve.wait_ge(h_out_ready, s)
                    dve.bn_stats(stats2[:, :], h_out[1 - par][:, :]).then_inc(stats2_done, 1)
                    dve.wait_ge(stats2_done, s)
                if active(3):
                    b = s - 3
                    dve.wait_ge(gate_done, b + 1)
                    dst = (scores_all[:, b, :] if isinstance(b, int)
                           else scores_all[:, bass.ds(b, 1), :].rearrange("p a e -> p (a e)"))
                    dve.tensor_copy(dst, ps_gate[1 - par]).then_inc(gate_copied, 1)
                if active(1):
                    dve.bn_aggr(mv2[:, :], stats2[:, :]).then_inc(aggr2, 1)
                    dve.wait_ge(aggr2, s)
                    dve.tensor_scalar(mv2[:, 1:2], mv2[:, 1:2], EPS, None, ALU.add).then_inc(mv2_done, 1)
            run(dve, body)


def route_and_experts(nc, outer, sb, ps, sem, env):
    fp32, i32, ALU, ACT, AX = env["fp32"], env["i32"], env["ALU"], env["ACT"], env["AX"]
    out, slot_rows = env["out"], env["slot_rows"]
    rows, scores_all, ident = env["rows"], env["scores_all"], env["ident"]

    NT = TOKEN_TILES
    ctx = ExitStack()
    with ctx:
        W12 = sb(ctx, "W12", [P, E * DK * 2 * HID])
        W3 = sb(ctx, "W3", [P, E * HK * D])
        tie_rank = sb(ctx, "tie_rank", [P, E])
        before = sb(ctx, "before", [P, P])
        ones = sb(ctx, "ones", [P, P])
        iota_i = sb(ctx, "iota_i", [P, P], i32)
        token_i = sb(ctx, "token_i", [P, NT], i32)
        first = [sb(ctx, f"first{n}", [P, NT, E]) for n in range(TOP)]
        work = sb(ctx, "work", [P, NT, E])
        work2 = sb(ctx, "work2", [P, NT, E])
        rest = sb(ctx, "rest", [P, NT, E])
        top = [sb(ctx, f"top{n}", [P, NT]) for n in range(TOP)]
        small = sb(ctx, "small", [P, NT])
        both = sb(ctx, "both", [P, NT, E])
        running = sb(ctx, "running", [P, NT, E])
        count_i = sb(ctx, "count_i", [P, E], i32)
        tiles_f = sb(ctx, "tiles_f", [P, E])
        tile_end = sb(ctx, "tile_end", [P, E])
        tile_start = sb(ctx, "tile_start", [P, E])
        slot_f = sb(ctx, "slot_f", [P, TOP, NT])
        slot_i = sb(ctx, "slot_i", [P, TOP, NT], i32)
        tile_no = sb(ctx, "tile_no", [1, TILES])
        tile_expert = sb(ctx, "tile_expert", [1, TILES])
        tile_expert_i = sb(ctx, "tile_expert_i", [1, TILES], i32)
        trash_row = sb(ctx, "trash_row", [P, 1])
        my_slot = [sb(ctx, f"my_slot{n}", [P, 1]) for n in range(2)]

        x_in = [sb(ctx, f"x_in{n}", [P, REC]) for n in range(2)]
        x_t = [sb(ctx, f"x_t{n}", [P, DK, P]) for n in range(2)]
        gated = sb(ctx, "gated", [P, HID])
        hidden = [sb(ctx, f"hidden{n}", [P, HID]) for n in range(2)]
        hidden_t = [sb(ctx, f"hidden_t{n}", [P, HK, P]) for n in range(1)]
        y_sb = [sb(ctx, f"y_sb{n}", [P, D]) for n in range(2)]
        is_first = sb(ctx, "is_first", [P, 1])
        second_p = sb(ctx, "second_p", [P, 1])
        weight = [sb(ctx, f"weight{n}", [P, 1]) for n in range(2)]
        pad_row = sb(ctx, "pad_row", [P, 1])
        dest = [sb(ctx, f"dest{n}", [P, 1], i32) for n in range(2)]

        ps_xt = ps(ctx, "ps_xt_moe", [P, DK, P])
        ps_h = [ps(ctx, f"ps_h{n}", [P, 2, HID]) for n in range(2)]
        ps_ht = ps(ctx, "ps_ht", [P, HK, P])
        ps_y = ps(ctx, "ps_y", [P, 512])
        ps_prefix = ps_h[0][:, 0, 0:TOKEN_TILES * E]
        ps_total = ps_h[0][:, 1, 0:TOKEN_TILES * E]

        weights_in = sem("weights_in")
        made = sem("route_consts")
        chain = sem("route_chain")
        both_ready, prefix_done = sem("both_ready"), sem("prefix_done")
        gap_ready, gap_exp = sem("gap_ready"), sem("gap_exp")
        slots_ready, tile_expert_ready = sem("slots_ready"), sem("tile_expert_ready")
        scattered = sem("scattered")
        x_loaded = [sem(f"x_loaded{n}") for n in range(2)]
        xt_done, xt_copied = sem("moe_xt_done"), sem("moe_xt_copied")
        h_done, silu_done, hidden_ready = sem("h_done"), sem("silu_done"), sem("hidden_ready")
        ht_done, ht_copied = sem("ht_done"), sem("ht_copied")
        y_done, y_ready = sem("y_done"), sem("y_ready")
        first_known, second_known, weight_known, pad_known, dest_known, slot_moved = (
            sem("first_known"), sem("second_known"), sem("weight_known"), sem("pad_known"), sem("dest_known"),
            sem("slot_moved"))
        y_added = sem("y_added")

        HEAD, END, ALL = 4, TILES, TILES + 2
        block = ctx.enter_context(nc.Block())

        @block.gpsimd
        def _(pool):
            pool.iota(token_i[:, :], pattern=[[P, NT]], base=1, channel_multiplier=1).then_inc(made, 1)
            pool.iota(iota_i[:, 0:E], pattern=[[-1, E]], base=E, channel_multiplier=0).then_inc(made, 1)
            pool.iota(iota_i[:, E:E + TILES], pattern=[[1, TILES]], base=0, channel_multiplier=0).then_inc(made, 1)
            pool.iota(iota_i[:, P - 1:P], pattern=[[0, 1]], base=0, channel_multiplier=1).then_inc(made, 1)
            pool.memset(ones[:, :], 1.0).then_inc(made, 1)
            pool.wait_ge(made, 5)
            pool.affine_select(out=before[:, :], in_=ones[:, :], compare_op=ALU.is_gt, fill=0.0, base=0,
                               pattern=[[1, P]], channel_multiplier=-1).then_inc(made, 1)
            pool.wait_ge(slots_ready, 1)
            for b in range(NT):
                real = min(P, TOKENS - b * P)
                for n in range(TOP):
                    pool.indirect_dma_start(
                        out=slot_rows[:, :],
                        out_offset=bass.IndirectOffsetOnAxis(ap=slot_i[0:real, n, b:b + 1], axis=0),
                        in_=rows[0:real, b, :], in_offset=None, bounds_check=SLOTS - 1).then_inc(scattered, 16)

            last_row = pool.to_reg(OUT_ROWS - 1)

            def body(s, par, active):
                if active(2):
                    t = s - 2
                    added = 16 * t if isinstance(t, int) else pool.to_reg(t * 16)
                    done = t + 1 if isinstance(t, int) else pool.to_reg(t + 1)
                    pool.wait_ge(slots_ready, 1)
                    after(pool, y_added, added)
                    pool.wait_ge(y_ready, done)
                    pool.wait_ge(dest_known, done)
                    pool.indirect_dma_start(
                        out=out[:, :], out_offset=bass.IndirectOffsetOnAxis(ap=dest[par][:, 0:1], axis=0),
                        in_=y_sb[par][:, :], in_offset=None, bounds_check=last_row,
                        compute_op=ALU.add).then_inc(y_added, 16)

            peeled = run_steps(pool, body, HEAD, END, TILES)
            for s in range(END, ALL):
                peeled(s, TILES)
            pool.wait_ge(y_added, 16 * TILES)

        @block.sync
        def _(sp):
            sp.wait_ge(scattered, 16 * NT * TOP)

            def body(s, par, active):
                if active(0):
                    after(sp, xt_done, s - 1)
                    after(sp, dest_known, s - 1)
                    after(sp, weight_known, s - 1)
                    src = slot_rows[s * P:(s + 1) * P, :] if isinstance(s, int) else slot_rows[bass.ds(s * P, P), :]
                    sp.dma_start(x_in[par][:, :], src).then_inc(x_loaded[par], 16)

            peeled = run_steps(sp, body, HEAD, END, TILES)

        @block.vector
        def _(dve):
            links = [0]

            def link(ins):
                links[0] += 1
                ins.then_inc(chain, 1)
                dve.wait_ge(chain, links[0])

            def per_expert(ap):
                return ap.unsqueeze(2).to_broadcast([P, NT, E])

            dve.wait_ge(made, 6)
            link(dve.tensor_copy(tie_rank[:, :], iota_i[:, 0:E]))
            link(dve.tensor_copy(tile_no[:, :], iota_i[0:1, E:E + TILES]))
            link(dve.tensor_scalar(trash_row[:, :], iota_i[:, P - 1:P], float(TOKENS + 1), None, ALU.add))
            for n in range(2):
                link(dve.tensor_scalar(my_slot[n][:, :], iota_i[:, P - 1:P], float(n * P), None, ALU.add))

            ranks = tie_rank[:, :].unsqueeze(1).to_broadcast([P, NT, E])
            scores = scores_all
            for n in range(TOP):
                link(dve.tensor_reduce(top[n][:, :], scores[:, :, :], AX.X, ALU.max))
                link(dve.tensor_tensor(work[:, :, :], scores[:, :, :], per_expert(top[n][:, :]), ALU.is_equal))
                link(dve.tensor_tensor(work[:, :, :], work[:, :, :], ranks, ALU.mult))
                link(dve.tensor_reduce(small[:, :], work[:, :, :], AX.X, ALU.max))
                link(dve.tensor_tensor(first[n][:, :, :], work[:, :, :], per_expert(small[:, :]), ALU.is_equal))
                if n == 0:
                    link(dve.scalar_tensor_tensor(rest[:, :, :], first[0][:, :, :], MASKED, scores_all[:, :, :],
                                                  ALU.mult, ALU.add))
                    scores = rest
            link(dve.tensor_tensor(both[:, :, :], first[0][:, :, :], first[1][:, :, :], ALU.add))
            dve.memset(both[TOKENS - (NT - 1) * P:P, NT - 1, :], 0.0).then_inc(both_ready, 1)
            dve.tensor_tensor(small[:, :], top[1][:, :], top[0][:, :], ALU.subtract).then_inc(gap_ready, 1)
            dve.wait_ge(gap_exp, 1)
            link(dve.tensor_scalar(top[0][:, :], small[:, :], 1.0, None, ALU.add))
            link(dve.reciprocal(top[1][:, :], top[0][:, :]))
            link(dve.tensor_copy(rows[:, :, REC_P1], top[1][:, :]))
            link(dve.tensor_tensor(rows[:, :, REC_P2], top[1][:, :], small[:, :], ALU.mult))
            link(dve.tensor_copy(rows[:, :, REC_ID], token_i[:, :]))

            dve.wait_ge(prefix_done, 1)
            link(dve.tensor_copy(work[:, :, :], ps_total.rearrange("p (b e) -> p b e", e=E)))
            for e in range(E):
                last = dve.tensor_tensor_scan(running[:, :, e], ones[:, 0:NT], work[:, :, e], 0.0, ALU.mult, ALU.add)
            link(last)
            link(dve.tensor_scalar(count_i[:, :], running[:, NT - 1, :], float(P - 1), None, ALU.add))
            link(dve.tensor_scalar(count_i[:, :], count_i[:, :], P.bit_length() - 1, None, ALU.arith_shift_right))
            link(dve.tensor_copy(tiles_f[:, :], count_i[:, :]))
            link(dve.tensor_tensor_scan(tile_end[:, :], ones[:, 0:E], tiles_f[:, :], 0.0, ALU.mult, ALU.add))
            link(dve.tensor_tensor(tile_start[:, :], tile_end[:, :], tiles_f[:, :], ALU.subtract))
            link(dve.tensor_scalar(tiles_f[:, :], tile_start[:, :], float(P), None, ALU.mult))
            link(dve.tensor_tensor(work2[:, :, :], running[:, :, :], work[:, :, :], ALU.subtract))
            link(dve.tensor_tensor(work2[:, :, :], work2[:, :, :], ps_prefix.rearrange("p (b e) -> p b e", e=E), ALU.add))
            link(dve.tensor_tensor(work2[:, :, :], work2[:, :, :],
                                   tiles_f[:, :].unsqueeze(1).to_broadcast([P, NT, E]), ALU.add))
            for n in range(TOP):
                link(dve.tensor_tensor(work[:, :, :], work2[:, :, :], first[n][:, :, :], ALU.mult))
                link(dve.tensor_reduce(slot_f[:, n, :], work[:, :, :], AX.X, ALU.add))
            link(dve.tensor_copy(rows[:, :, REC_SLOT], slot_f[:, 0, :]))
            dve.tensor_copy(slot_i[:, :, :], slot_f[:, :, :]).then_inc(slots_ready, 1)
            link(dve.tensor_scalar(tile_expert[:, :], tile_no[:, :], tile_start[0:1, 1:2], None, ALU.is_ge))
            for e in range(2, E):
                link(dve.scalar_tensor_tensor(tile_expert[:, :], tile_no[:, :], tile_start[0:1, e:e + 1],
                                              tile_expert[:, :], ALU.is_ge, ALU.add))
            dve.tensor_copy(tile_expert_i[:, :], tile_expert[:, :]).then_inc(tile_expert_ready, 1)

            def body(s, par, active):
                if active(1):
                    t = s - 1
                    x, mine = x_in[1 - par], my_slot[1 - par]
                    dve.wait_ge(x_loaded[1 - par], 16 * (t // 2 + 1) if isinstance(t, int) else (t - (1 - par) + 2) * 8)
                    after(dve, slot_moved, t - 1)
                    after(dve, weight_known, t)
                    after(dve, dest_known, t)
                    dve.tensor_scalar(is_first[:, :], x[:, REC_SLOT:REC_SLOT + 1], mine[:, 0:1], None,
                                      ALU.is_equal).then_inc(first_known, 1)
                    dve.wait_ge(first_known, t + 1)
                    dve.tensor_scalar(second_p[:, :], is_first[:, :], 0.0, x[:, REC_P2:REC_P2 + 1], ALU.is_equal,
                                      ALU.mult).then_inc(second_known, 1)
                    dve.tensor_scalar(pad_row[:, :], x[:, REC_ID:REC_ID + 1], 0.0, trash_row[:, 0:1], ALU.is_equal,
                                      ALU.mult).then_inc(pad_known, 1)
                    dve.tensor_scalar(mine[:, :], mine[:, :], float(2 * P), None, ALU.add).then_inc(slot_moved, 1)
                    dve.wait_ge(second_known, t + 1)
                    dve.scalar_tensor_tensor(weight[1 - par][:, :], is_first[:, :], x[:, REC_P1:REC_P1 + 1],
                                             second_p[:, :], ALU.mult, ALU.add).then_inc(weight_known, 1)
                    dve.wait_ge(pad_known, t + 1)
                    after(dve, y_added, 16 * (t - 1) if isinstance(t, int) else (t - 1) * 16)
                    dve.scalar_tensor_tensor(dest[1 - par][:, :], pad_row[:, :], -1.0, x[:, REC_ID:REC_ID + 1],
                                             ALU.add, ALU.add).then_inc(dest_known, 1)
                if active(1):
                    t = s - 1
                    dve.wait_ge(silu_done, t + 1)
                    after(dve, ht_done, t - 1)
                    dve.tensor_tensor(hidden[1 - par][:, :], gated[:, :], ps_h[1 - par][:, 1, :],
                                      ALU.mult).then_inc(hidden_ready, 1)
                if active(2):
                    t = s - 2
                    dve.wait_ge(y_done, t + 1)
                    dve.wait_ge(weight_known, t + 1)
                    after(dve, y_added, 16 * (t - 1) if isinstance(t, int) else (t - 1) * 16)
                    dve.tensor_scalar(y_sb[par][:, :], ps_y[:, 0:D], weight[par][:, 0:1], None,
                                      ALU.mult).then_inc(y_ready, 1)

            peeled = run_steps(dve, body, HEAD, END, TILES)
            for s in range(END, ALL):
                peeled(s, TILES)

        @block.scalar
        def _(act):
            for e in range(E):
                act.dma_start(W12[:, e * DK * 2 * HID:(e + 1) * DK * 2 * HID].rearrange("p (k h) -> p k h", k=DK),
                              env["w12"][e].rearrange("(k p) h -> p k h", p=P)).then_inc(weights_in, 16)
                act.dma_start(W3[:, e * HK * D:(e + 1) * HK * D].rearrange("p (c d) -> p c d", c=HK),
                              env["w3"][e].rearrange("(c p) d -> p c d", p=P)).then_inc(weights_in, 16)
            act.wait_ge(gap_ready, 1)
            act.activation(small[:, :], small[:, :], ACT.Exp).then_inc(gap_exp, 1)

            def body(s, par, active):
                if active(0):
                    act.wait_ge(xt_done, s + 1)
                    after(act, h_done, s - 1)
                    act.activation(x_t[par][:, :, :], ps_xt[:, :, :], ACT.Copy).then_inc(xt_copied, 1)
                if active(2):
                    act.wait_ge(ht_done, s - 1)
                    act.activation(hidden_t[0][:, :, :], ps_ht[:, :, :], ACT.Copy).then_inc(ht_copied, 1)
                if active(1):
                    act.wait_ge(h_done, s)
                    after(act, hidden_ready, s - 1)
                    act.activation(gated[:, :], ps_h[1 - par][:, 0, :], ACT.Silu).then_inc(silu_done, 1)

            peeled = run_steps(act, body, HEAD, END, TILES)
            for s in range(END, ALL):
                peeled(s, TILES)

        @block.tensor
        def _(pe):
            pe.wait_ge(both_ready, 1)
            pe.wait_ge(made, 6)
            choice = both[:, :, :].rearrange("p b e -> p (b e)")
            pe.matmul(ps_prefix, before[:, :], choice, start=True, stop=True)
            pe.matmul(ps_total, ones[:, :], choice, start=True, stop=True).then_inc(prefix_done, 1)
            pe.wait_ge(slots_ready, 1)
            pe.wait_ge(tile_expert_ready, 1)
            pe.wait_ge(weights_in, 16 * 2 * E)

            def body(s, par, active):
                if active(1):
                    up_expert = expert_of(s - 1)
                if active(2):
                    down_expert = expert_of(s - 2)
                if active(0):
                    pe.wait_ge(x_loaded[par], 16 * (s // 2 + 1) if isinstance(s, int) else (s - par + 2) * 8)
                    after(pe, xt_copied, s)
                    for k in range(DK):
                        mm = pe.transpose(ps_xt[:, k, :], x_in[par][:, k * P:(k + 1) * P], ident[:, :])
                    mm.then_inc(xt_done, 1)
                if active(2):
                    pe.wait_ge(hidden_ready, s - 1)
                    for c in range(HK):
                        mm = pe.transpose(ps_ht[:, c, :], hidden[par][:, c * P:(c + 1) * P], ident[:, :])
                    mm.then_inc(ht_done, 1)
                if active(1):
                    t = s - 1
                    pe.wait_ge(xt_copied, t + 1)
                    after(pe, hidden_ready, t - 1)
                    for half in range(2):
                        for k in range(DK):
                            mm = pe.matmul(ps_h[1 - par][:, half, :], x_t[1 - par][:, k, :],
                                           W12[:, bass.ds(up_expert * (DK * 2 * HID) + (k * 2 + half) * HID, HID)],
                                           start=(k == 0), stop=(k == DK - 1))
                    mm.then_inc(h_done, 1)
                if active(2):
                    t = s - 2
                    pe.wait_ge(ht_copied, t + 1)
                    after(pe, y_ready, t)
                    for c in range(HK):
                        mm = pe.matmul(ps_y[:, 0:D], hidden_t[0][:, c, :],
                                       W3[:, bass.ds(down_expert * (HK * D) + c * D, D)],
                                       start=(c == 0), stop=(c == HK - 1))
                    mm.then_inc(y_done, 1)

            def expert_of(t):
                at = tile_expert_i[0:1, t:t + 1] if isinstance(t, int) else tile_expert_i[0:1, bass.ds(t, 1)]
                return pe.value_load(at, min_val=0, max_val=E - 1)

            peeled = run_steps(pe, body, HEAD, END, TILES)
            for s in range(END, ALL):
                peeled(s, TILES)


def kernel(**inputs):
    import numpy as np
    import concourse.bacc as bacc
    from concourse import mybir as mb
    from concourse.bass_utils import run_bass_kernel_spmd

    a = {k: np.asarray(v) for k, v in inputs.items()}
    side = 16
    grid = 6
    x = a["x"].reshape(BATCH, 3, grid, side, grid, side)
    arrays = {
        "patches": x.transpose(1, 3, 5, 0, 2, 4).reshape(F, IMG_TOKENS),
        "txt": a["txt"].reshape(BATCH * TXT, D),
        "w_lin": a["L0_tok_W_lin"].T,
        "b_lin": a["L0_tok_b_lin"].reshape(1, D),
        "cls": a["L0_tok_class_token"].reshape(1, D),
        "pos": a["L0_tok_position_embeddings"].reshape(1 + IMG, D),
        "w_down": np.concatenate([a["L0_attn_W_dq"], a["L0_attn_W_dkv"]], axis=1),
        "gamma": np.concatenate([a["L0_attn_q_ln_g"], a["L0_attn_kv_ln_g"]]).reshape(P, 1),
        "beta": np.concatenate([a["L0_attn_q_ln_b"], a["L0_attn_kv_ln_b"]]).reshape(P, 1),
        "w_uq": a["L0_attn_W_uq"],
        "w_ukv": a["L0_attn_W_ukv"],
        "w_o": a["L0_attn_W_o"].T,
        "w12": a["L0_ffn_w12"].transpose(0, 2, 1),
        "w3": a["L0_ffn_w3"].transpose(0, 2, 1),
        "gate": a["L0_ffn_gate_w"].T,
    }
    arrays = {k: np.ascontiguousarray(v) for k, v in arrays.items()}
    nc = bacc.Bacc("TRN2", target_bir_lowering=False, num_devices=1)
    args = {k: nc.dram_tensor(k, v.shape, mb.dt.from_np(v.dtype), kind="ExternalInput").ap() for k, v in arrays.items()}
    out = nc.dram_tensor("out", [OUT_ROWS, D], mb.dt.float32, kind="ExternalOutput").ap()
    build(nc, out=out, **args)
    r = run_bass_kernel_spmd(nc, [arrays], core_ids=[0])
    return r.results[0]["out"][0:TOKENS].reshape(BATCH, S, D)
```

```python
import concourse.bass as bass
from concourse import mybir
from contextlib import ExitStack

P = 128
BATCH, IMG, TXT = 64, 36, 32
S = 1 + IMG + TXT
TOKENS = BATCH * S
TOKEN_TILES = -(-TOKENS // P)
PADDED = TOKEN_TILES * P
D = 256
F = 768
FK = F // P
DK = D // P
IMG_TOKENS = BATCH * IMG
PER_TILE = P // IMG
EMB = PER_TILE * IMG
IMG_TILES = -(-BATCH // PER_TILE)
HEADS, DH = 16, 16
GROUPS = 4
UNITS = HEADS // GROUPS
PAIR = 2 * S
PROJ = D // 4
E = 8
TOP = 2
HID = 512
HK = HID // P
TILES = (TOKENS * TOP - E) // P + E
OUT_ROWS = TOKENS + P
EPS = 1e-5
UNROLL = 8
MASKED = -1e30


def build(nc, patches, txt, w_lin, b_lin, cls, pos, w_down, gamma, beta, w_uq, w_ukv, w_o, w12, w3, gate, out):
    fp32 = mybir.dt.float32
    i32 = mybir.dt.int32
    ALU = mybir.AluOpType
    ACT = mybir.ActivationFunctionType
    AX = mybir.AxisListType

    h_rows = nc.dram_tensor("h_rows", [PADDED, D], fp32, kind="Internal").ap()
    normed_rows = nc.dram_tensor("normed_rows", [PADDED, D], fp32, kind="Internal").ap()

    ctx = ExitStack()
    with ctx:
        def sem(name):
            return ctx.enter_context(nc.semaphore(name))

        def sb(stack, name, shape, dt=fp32):
            return stack.enter_context(nc.sbuf_tensor(name, shape, dt))

        def ps(stack, name, shape, dt=fp32):
            return stack.enter_context(nc.psum_tensor(name, shape, dt))

        W3 = sb(ctx, "W3", [P, E * HK * D])
        W12 = [sb(ctx, "W12_0", [P, E * 2 * HID])]
        scores_all = sb(ctx, "scores_all", [P, TOKEN_TILES, E])
        ident = sb(ctx, "ident", [P, P])
        consts_ready = sem("consts_ready")
        pads_cleared = sem("pads_cleared")

        until_gate(nc, sb, ps, sem, locals())
        route_and_experts(nc, ctx, sb, ps, sem, locals())


def until_gate(nc, sb, ps, sem, env):
    with ExitStack() as ctx:
        w_down_sb = sb(ctx, "w_down_sb", [P, DK, P])
        gamma_sb = sb(ctx, "gamma_sb", [P, 1])
        beta_sb = sb(ctx, "beta_sb", [P, 1])
        w_qk = [sb(ctx, f"w_qk{n}", [P, UNITS, P]) for n in range(2)]
        w_v = sb(ctx, "w_v", [P, D])
        w_o_sb = sb(ctx, "w_o_sb", [P, DK, D])
        gate_sb = sb(ctx, "gate_sb", [P, DK, E])
        minus_half = sb(ctx, "minus_half", [P, 2])
        zero_rows = sb(ctx, "zero_rows", [P, D])
        c_t = sb(ctx, "c_t", [P, PADDED])
        rows = sb(ctx, "rows", [P, TOKEN_TILES, D])
        o_t = sb(ctx, "o_t", [P, DK, PADDED])
        k_diag = sb(ctx, "k_diag", [P, UNITS, GROUPS, PAIR])
        v_sb = [sb(ctx, f"v_sb{n}", [S, HEADS, DH + 1]) for n in range(2)]
        env = {**env, **locals()}
        embed(nc, sb, ps, sem, env)
        compress(nc, sb, ps, sem, env)
        attention(nc, sb, ps, sem, env)
        output(nc, sb, ps, sem, env)


def after(eng, semaphore, value):
    if not (isinstance(value, int) and value <= 0):
        eng.wait_ge(semaphore, value)


def run_steps(eng, body, head, end, total, cycle=2):
    def peeled(n, count):
        body(n, n % cycle, lambda k: 0 <= n - k < count)

    for n in range(head):
        peeled(n, total)
    assert (end - head) % UNROLL == 0 and UNROLL % cycle == 0
    with eng.Fori(0, (end - head) // UNROLL) as i:
        for j in range(UNROLL):
            body(i * UNROLL + (head + j), (head + j) % cycle, lambda k: True)
    return peeled


def parity_count(unit, s, par):
    return 16 * unit * (s // 2 + 1) if isinstance(s, int) else (s - par + 2) * (8 * unit)


def row_of(rows, t):
    if isinstance(t, int):
        return rows[:, t, 0:D]
    return rows[:, bass.ds(t, 1), 0:D].rearrange("p a d -> p (a d)")


def embed(nc, sb, ps, sem, env):
    ALU = env["ALU"]
    patches, txt, h_rows, ident = (env[n] for n in ("patches", "txt", "h_rows", "ident"))
    w_down_sb, gamma_sb, beta_sb, w_qk, w_v, w_o_sb, gate_sb, minus_half, o_t, k_diag, v_sb = (
        env[n] for n in ("w_down_sb", "gamma_sb", "beta_sb", "w_qk", "w_v", "w_o_sb", "gate_sb", "minus_half",
                         "o_t", "k_diag", "v_sb"))
    consts_ready, zero_rows = env["consts_ready"], env["zero_rows"]
    by_batch = h_rows[0:TOKENS, :].rearrange("(b s) d -> b s d", s=S)
    with ExitStack() as ctx:
        w_lin_sb = sb(ctx, "w_lin_sb", [P, FK, D])
        patch_sb = [sb(ctx, f"patch_sb{n}", [P, FK * EMB]) for n in range(3)]
        emb_sb = [sb(ctx, f"emb_sb{n}", [EMB, D]) for n in range(2)]
        base_sb = sb(ctx, "base_sb", [EMB, D])
        img_pos_sb = sb(ctx, "img_pos_sb", [EMB, D])
        cls_sb = sb(ctx, "cls_sb", [BATCH, D])
        cls_pos_sb = sb(ctx, "cls_pos_sb", [BATCH, D])
        ps_emb = [ps(ctx, f"ps_emb{n}", [P, 512])[0:EMB, 0:D] for n in range(2)]
        patch_in = [sem(f"patch_in{n}") for n in range(3)]
        w_lin_in, small_in, base_in = sem("w_lin_in"), sem("small_in"), sem("base_in")
        emb_mm, emb_added = sem("emb_mm"), sem("emb_added")
        emb_stored = [sem(f"emb_stored{n}") for n in range(2)]
        base_ready, rows_laid, zeros_made = sem("base_ready"), sem("rows_laid"), sem("zeros_made")
        rows_padded = sem("rows_padded")
        SMALL = 8
        block = ctx.enter_context(nc.Block())

        def batches(t):
            return min(PER_TILE, BATCH - t * PER_TILE)

        @block.sync
        def _(sp):
            sp.dma_start(w_lin_sb[:, :, :], env["w_lin"].rearrange("(k p) d -> p k d", p=P)).then_inc(w_lin_in, 16)
            for t in range(IMG_TILES):
                n = batches(t) * IMG
                if t >= 3:
                    sp.wait_ge(emb_mm, t - 2)
                at = t * FK * EMB
                sp.dma_start(patch_sb[t % 3][:, 0:FK * n], patches[:, at:at + FK * n]).then_inc(patch_in[t % 3], 16)
                if t == 1:
                    sp.dma_start(w_down_sb[:, :, :],
                                 env["w_down"].rearrange("(k p) d -> p k d", p=P)).then_inc(small_in, 16)
                    sp.dma_start(gamma_sb[:, :], env["gamma"]).then_inc(small_in, 16)
                    sp.dma_start(beta_sb[:, :], env["beta"]).then_inc(small_in, 16)
                    sp.wait_ge(zeros_made, 3)
                    spread = [w[:, :, :].rearrange("p u (g d) -> p (u g) d", g=GROUPS) for w in w_qk]
                    sp.dma_start(spread[0][0:PROJ, :, 0:DH],
                                 env["w_uq"].rearrange("p (h d) -> p h d", d=DH)).then_inc(small_in, 16)
                    sp.dma_start(spread[1][PROJ:P, :, 0:DH],
                                 env["w_ukv"][:, 0:D].rearrange("p (h d) -> p h d", d=DH)).then_inc(small_in, 16)
                    sp.dma_start(w_v[PROJ:P, :], env["w_ukv"][:, D:2 * D]).then_inc(small_in, 16)
                    sp.dma_start(w_o_sb[:, :, :],
                                 env["w_o"].rearrange("(k p) d -> p k d", p=P)).then_inc(small_in, 16)
                    sp.dma_start(gate_sb[:, :, :],
                                 env["gate"].rearrange("(k p) e -> p k e", p=P)).then_inc(small_in, 16)
            sp.wait_ge(small_in, 16 * SMALL)

        @block.gpsimd
        def _(pool):
            for w in w_qk:
                pool.memset(w[:, :, :], 0.0).then_inc(zeros_made, 1)
            pool.memset(w_v[0:PROJ, :], 0.0).then_inc(zeros_made, 1)
            pool.memset(zero_rows[:, :], 0.0).then_inc(zeros_made, 1)
            pool.memset(minus_half[:, :], -0.5).then_inc(consts_ready, 1)
            for n in range(2):
                pool.memset(v_sb[n][:, :, :], 1.0).then_inc(consts_ready, 1)
            pool.memset(k_diag[:, :, :, :], 0.0).then_inc(consts_ready, 1)
            pool.memset(o_t[:, :, TOKENS:PADDED], 0.0).then_inc(consts_ready, 1)
            pool.memset(ident[:, :], 0.0).then_inc(consts_ready, 1)
            pool.wait_ge(consts_ready, 6)
            pool.affine_select(out=ident[:, :], in_=ident[:, :], compare_op=ALU.not_equal, fill=1.0, base=0,
                               pattern=[[-1, P]], channel_multiplier=1).then_inc(consts_ready, 1)
            pool.wait_ge(zeros_made, 4)
            pool.dma_start(h_rows[TOKENS:PADDED, :], zero_rows[0:PADDED - TOKENS, 0:D]).then_inc(rows_padded, 16)
            pool.wait_ge(rows_padded, 16)

        @block.scalar
        def _(act):
            act.dma_start(base_sb[:, :], env["b_lin"].to_broadcast([EMB, D])).then_inc(base_in, 16)
            for n in range(PER_TILE):
                act.dma_start(img_pos_sb[n * IMG:(n + 1) * IMG, :], env["pos"][1:1 + IMG, :]).then_inc(base_in, 16)
            act.dma_start(cls_sb[:, :], env["cls"].to_broadcast([BATCH, D])).then_inc(base_in, 16)
            act.dma_start(cls_pos_sb[:, :], env["pos"][0:1, :].to_broadcast([BATCH, D])).then_inc(base_in, 16)
            act.dma_start(by_batch[:, 1 + IMG:S, :], txt.rearrange("(b t) d -> b t d", t=TXT)).then_inc(rows_laid, 16)
            act.wait_ge(base_ready, 2)
            act.dma_start(by_batch[:, 0, :], cls_sb[:, :]).then_inc(rows_laid, 16)
            for t in range(IMG_TILES):
                act.wait_ge(emb_added, t + 1)
                for n in range(batches(t)):
                    act.dma_start(by_batch[t * PER_TILE + n, 1:1 + IMG, :],
                                  emb_sb[t % 2][n * IMG:(n + 1) * IMG, :]).then_inc(emb_stored[t % 2], 16)
            act.wait_ge(rows_laid, 32)
            for n in range(2):
                act.wait_ge(emb_stored[n], 16 * sum(batches(t) for t in range(n, IMG_TILES, 2)))

        @block.vector
        def _(dve):
            dve.wait_ge(base_in, 16 * (PER_TILE + 3))
            dve.tensor_tensor(base_sb[:, :], base_sb[:, :], img_pos_sb[:, :], ALU.add).then_inc(base_ready, 1)
            dve.tensor_tensor(cls_sb[:, :], cls_sb[:, :], cls_pos_sb[:, :], ALU.add).then_inc(base_ready, 1)
            dve.wait_ge(base_ready, 2)
            for t in range(IMG_TILES):
                n = batches(t) * IMG
                dve.wait_ge(emb_mm, t + 1)
                if t >= 2:
                    dve.wait_ge(emb_stored[t % 2], 16 * PER_TILE * (t // 2))
                dve.tensor_tensor(emb_sb[t % 2][0:n, :], ps_emb[t % 2][0:n, :], base_sb[0:n, :],
                                  ALU.add).then_inc(emb_added, 1)

        @block.tensor
        def _(pe):
            pe.wait_ge(w_lin_in, 16)
            for t in range(IMG_TILES):
                n = batches(t) * IMG
                pe.wait_ge(patch_in[t % 3], 16 * (t // 3 + 1))
                if t >= 2:
                    pe.wait_ge(emb_added, t - 1)
                for k in range(FK):
                    mm = pe.matmul(ps_emb[t % 2][0:n, :], patch_sb[t % 3][:, k * n:(k + 1) * n], w_lin_sb[:, k, :],
                                   start=(k == 0), stop=(k == FK - 1))
                mm.then_inc(emb_mm, 1)


def compress(nc, sb, ps, sem, env):
    ALU, ACT = env["ALU"], env["ACT"]
    h_rows, rows, ident, minus_half, w_down_sb, gamma_sb, beta_sb, c_t = (
        env[n] for n in ("h_rows", "rows", "ident", "minus_half", "w_down_sb", "gamma_sb", "beta_sb", "c_t"))
    with ExitStack() as ctx:
        stats1 = sb(ctx, "stats1", [P, 6])
        mv1 = [sb(ctx, f"mv1{n}", [P, 2]) for n in range(2)]
        rstd1 = [sb(ctx, f"rstd1{n}", [P, 1]) for n in range(2)]
        xn = [sb(ctx, f"xn{n}", [P, D]) for n in range(2)]
        xn_t = [sb(ctx, f"xn_t{n}", [P, DK, P]) for n in range(2)]
        stats_c = sb(ctx, "stats_c", [P, 2, 6])
        mv_c = [sb(ctx, f"mv_c{n}", [P, 2, 2]) for n in range(2)]
        rstd_c = [sb(ctx, f"rstd_c{n}", [P, 2]) for n in range(2)]
        cn = [sb(ctx, f"cn{n}", [P, P]) for n in range(2)]
        ps_xt = [ps(ctx, f"ps_xt{n}", [P, 512])[:, 0:D].rearrange("p (k s) -> p k s", k=DK) for n in range(2)]
        ps_down = [ps(ctx, f"ps_down{n}", [P, 512])[:, 0:P] for n in range(4)]
        ps_ct = [ps(ctx, f"ps_ct{n}", [P, 512])[:, 0:P] for n in range(2)]
        loaded = [sem(f"loaded{n}") for n in range(2)]
        stats1_done, aggr1, mv1_done, rstd1_done, xn_ready = (
            sem("stats1_done"), sem("aggr1"), sem("mv1_done"), sem("rstd1_done"), sem("xn_ready"))
        xt_done, xt_copied, down_done = sem("xt_done"), sem("xt_copied"), sem("down_done")
        stats_c_done, aggr_c, mv_c_done, rstd_c_done, cn_ready = (
            sem("stats_c_done"), sem("aggr_c"), sem("mv_c_done"), sem("rstd_c_done"), sem("cn_ready"))
        ct_done, ct_copied = sem("ct_done"), sem("ct_copied")
        N = TOKEN_TILES
        HEAD, ALL = 7, N + 4
        END = HEAD + (N - HEAD) // UNROLL * UNROLL
        block = ctx.enter_context(nc.Block())

        def run(eng, body):
            peeled = run_steps(eng, body, HEAD, END, N, cycle=4)
            for s in range(END, ALL):
                peeled(s, N)

        @block.sync
        def _(sp):
            def body(s, quarter, active):
                par = quarter % 2
                if active(0):
                    if not isinstance(s, int) or s >= 2:
                        sp.wait_ge(loaded[par], parity_count(1, s - 2, par))
                    src = h_rows[s * P:(s + 1) * P, :] if isinstance(s, int) else h_rows[bass.ds(s * P, P), :]
                    sp.dma_start(row_of(rows, s), src).then_inc(loaded[par], 16)
            run(sp, body)

        @block.gpsimd
        def _(pool):
            def body(s, quarter, active):
                par = quarter % 2
                if active(0):
                    pool.wait_ge(mv1_done, s + 1)
                    after(pool, xn_ready, s - 1)
                    pool.tensor_tensor(rstd1[par][:, :], mv1[par][:, 1:2], minus_half[:, 0:1], ALU.pow).then_inc(rstd1_done, 1)
                if active(2):
                    pool.wait_ge(mv_c_done, s - 1)
                    after(pool, cn_ready, s - 3)
                    pool.tensor_tensor(rstd_c[par][:, :], mv_c[par][:, :, 1], minus_half[:, :], ALU.pow).then_inc(rstd_c_done, 1)
            run(pool, body)

        @block.scalar
        def _(act):
            def body(s, quarter, active):
                par = quarter % 2
                if active(1):
                    act.wait_ge(xt_done, s)
                    after(act, down_done, s - 2)
                    act.activation(xn_t[1 - par][:, :, :], ps_xt[1 - par], ACT.Copy).then_inc(xt_copied, 1)
                if active(4):
                    act.wait_ge(ct_done, s - 3)
                    b = s - 4
                    dst = c_t[:, b * P:(b + 1) * P] if isinstance(b, int) else c_t[:, bass.ds(b * P, P)]
                    act.activation(dst, ps_ct[par], ACT.Identity, bias=beta_sb[:, 0:1],
                                   scale=gamma_sb[:, 0:1]).then_inc(ct_copied, 1)
            run(act, body)

        @block.tensor
        def _(pe):
            def body(s, quarter, active):
                par = quarter % 2
                if active(2):
                    pe.wait_ge(xt_copied, s - 1)
                    after(pe, cn_ready, s - 5)
                    for k in range(DK):
                        mm = pe.matmul(ps_down[(quarter - 2) % 4], xn_t[par][:, k, :], w_down_sb[:, k, :], start=(k == 0),
                                       stop=(k == DK - 1))
                    mm.then_inc(down_done, 1)
                if active(4):
                    pe.wait_ge(cn_ready, s - 3)
                    after(pe, ct_copied, s - 5)
                    pe.transpose(ps_ct[par], cn[par][:, :], ident[:, :]).then_inc(ct_done, 1)
                if active(1):
                    pe.wait_ge(xn_ready, s)
                    after(pe, xt_copied, s - 2)
                    for k in range(DK):
                        mm = pe.transpose(ps_xt[1 - par][:, k, :], xn[1 - par][:, k * P:(k + 1) * P], ident[:, :])
                    mm.then_inc(xt_done, 1)
            run(pe, body)

        @block.vector
        def _(dve):
            def body(s, quarter, active):
                par = quarter % 2
                if active(0):
                    dve.wait_ge(loaded[par], parity_count(1, s, par))
                    dve.bn_stats(stats1[:, :], row_of(rows, s)).then_inc(stats1_done, 1)
                    dve.wait_ge(stats1_done, s + 1)
                if active(1):
                    dve.wait_ge(rstd1_done, s)
                    after(dve, xt_done, s - 2)
                    dve.tensor_scalar(xn[1 - par][:, :], row_of(rows, s - 1), mv1[1 - par][:, 0:1],
                                      rstd1[1 - par][:, 0:1], ALU.subtract, ALU.mult).then_inc(xn_ready, 1)
                if active(0):
                    dve.bn_aggr(mv1[par][:, :], stats1[:, :]).then_inc(aggr1, 1)
                if active(2):
                    dve.wait_ge(down_done, s - 1)
                    for n in range(2):
                        stat = dve.bn_stats(stats_c[:, n, :], ps_down[(quarter - 2) % 4][:, n * PROJ:(n + 1) * PROJ])
                    stat.then_inc(stats_c_done, 1)
                if active(0):
                    dve.wait_ge(aggr1, s + 1)
                if active(2):
                    dve.wait_ge(stats_c_done, s - 1)
                if active(0):
                    dve.tensor_scalar(mv1[par][:, 1:2], mv1[par][:, 1:2], EPS, None, ALU.add).then_inc(mv1_done, 1)
                if active(2):
                    for n in range(2):
                        stat = dve.bn_aggr(mv_c[par][:, n, :], stats_c[:, n, :])
                    stat.then_inc(aggr_c, 1)
                if active(3):
                    dve.wait_ge(rstd_c_done, s - 2)
                    after(dve, ct_done, s - 4)
                    for n in range(2):
                        last = dve.tensor_scalar(cn[1 - par][:, n * PROJ:(n + 1) * PROJ],
                                                 ps_down[(quarter - 3) % 4][:, n * PROJ:(n + 1) * PROJ], mv_c[1 - par][:, n, 0:1],
                                                 rstd_c[1 - par][:, n:n + 1], ALU.subtract, ALU.mult)
                    last.then_inc(cn_ready, 1)
                if active(2):
                    dve.wait_ge(aggr_c, s - 1)
                    dve.tensor_scalar(mv_c[par][:, :, 1], mv_c[par][:, :, 1], EPS, None, ALU.add).then_inc(mv_c_done, 1)
            run(dve, body)


def attention(nc, sb, ps, sem, env):
    ALU, ACT, AX = env["ALU"], env["ACT"], env["AX"]
    w_qk, w_v, c_t, o_t, k_diag, v_sb, ident = (
        env[n] for n in ("w_qk", "w_v", "c_t", "o_t", "k_diag", "v_sb", "ident"))
    with ExitStack() as ctx:
        c_pair = [sb(ctx, f"c_pair{n}", [P, PAIR]) for n in range(2)]
        q_t = sb(ctx, "q_t", [P, UNITS, PAIR])
        scores = [sb(ctx, f"scores{n}", [S, HEADS, S]) for n in range(2)]
        probs = [sb(ctx, f"probs{n}", [S, HEADS, S]) for n in range(2)]
        zeros_out = sb(ctx, "zeros_out", [S, HEADS, S])
        row_max = sb(ctx, "row_max", [S, HEADS])
        p_t = [sb(ctx, f"p_t{n}", [S, GROUPS * S]) for n in range(2)]
        inv_sum = sb(ctx, "inv_sum", [S, HEADS])
        o_norm = sb(ctx, "o_norm", [S, HEADS, DH])
        ps_scores = ps(ctx, "ps_scores", [P, UNITS, 512])
        ps_pt = [ps(ctx, f"ps_pt{n}", [P, 512]) for n in range(2)]
        ps_out = ps(ctx, "ps_out", [P, 512])
        ps_v = ps(ctx, "ps_v", [P, 512])[0:S, 0:D]
        ps_o = ps_out[0:S, 0:HEADS * (DH + 1)].rearrange("p (h d) -> p h d", h=HEADS)
        ps_ot = ps_out[:, HEADS * (DH + 1):HEADS * (DH + 1) + DK * S].rearrange("p (k s) -> p k s", k=DK)

        pair_ready = sem("pair_ready")
        k_copied = sem("k_copied")
        qk_done, q_copied = sem("qk_done"), sem("q_copied")
        v_done, v_copied = sem("v_done"), sem("v_copied")
        scores_done, scores_copied, causal_done = sem("scores_done"), sem("scores_copied"), sem("causal_done")
        upper_copied = sem("upper_copied")
        zero_marked, zero_masked, max_done, shifted, exp_done = (
            sem("zero_marked"), sem("zero_masked"), sem("max_done"), sem("shifted"), sem("exp_done"))
        pt_done, pt_copied, pv_unit = sem("pt_done"), sem("pt_copied"), sem("pv_unit")
        inv_done, o_ready, ot_done, ot_copied = sem("inv_done"), sem("o_ready"), sem("ot_done"), sem("ot_copied")
        HEAD, END, ALL = 8, BATCH, BATCH + 4
        block = ctx.enter_context(nc.Block())

        def run(eng, body):
            peeled = run_steps(eng, body, HEAD, END, BATCH, cycle=4)
            for s in range(END, ALL):
                peeled(s, BATCH)

        @block.sync
        def _(sp):
            out, zero_rows, pads_cleared = (env[n] for n in ("out", "zero_rows", "pads_cleared"))
            W3, early_in = env["W3"], sem("early_in")
            for e in range(E):
                sp.dma_start(W3[:, e * HK * D:(e + 1) * HK * D].rearrange("p (c d) -> p c d", c=HK),
                             env["w3"][e].rearrange("(c p) d -> p c d", p=P)).then_inc(early_in, 16)
                sp.dma_start(env["W12"][0][:, e * 2 * HID:(e + 1) * 2 * HID],
                             env["w12"][e, 0:P, :]).then_inc(early_in, 16)
            sp.wait_ge(early_in, 16 * E * 2)
            sp.dma_start(out[PADDED:OUT_ROWS, :], zero_rows[0:OUT_ROWS - PADDED, 0:D]).then_inc(pads_cleared, 16)
            sp.wait_ge(pads_cleared, 16)

        @block.gpsimd
        def _(pool):
            masked = pool.to_reg(MASKED)

            def body(s, quarter, active):
                par = quarter % 2
                if active(0) and par == 0:
                    after(pool, v_done, s - 2)
                    src = c_t[:, s * S:s * S + PAIR] if isinstance(s, int) else c_t[:, bass.ds(s * S, PAIR)]
                    pool.tensor_copy(c_pair[quarter // 2][:, :], src).then_inc(pair_ready, 2)
                if active(1):
                    copied = s if isinstance(s, int) else pool.to_reg(s)

                    pool.wait_ge(env["consts_ready"], 7)
                    pool.wait_ge(scores_copied, copied)
                    sc = scores[1 - par]
                    pool.affine_select(out=sc[:, :, :], in_=sc[:, :, :], compare_op=ALU.is_ge, fill=masked, base=0,
                                       pattern=[[0, HEADS], [-1, S]], channel_multiplier=1).then_inc(causal_done, 1)

            run(pool, body)

        def key_block(eng_copy, g):
            part = slice(32 * g, 32 * g + 32)
            return eng_copy(k_diag[part, :, g, :].rearrange("p (a u) s -> p a u s", a=2),
                            ps_scores[part, 2:4, 0:2 * PAIR].rearrange("p a (u s) -> p a u s", u=2))

        ON_ACT = 3

        @block.scalar
        def _(act):
            def body(s, quarter, active):
                par = quarter % 2
                def copy_turned(u):
                    n = (s - 3) * UNITS + u
                    act.wait_ge(pt_done, n + 1)
                    after(act, pv_unit, n - 1)
                    act.activation(p_t[u % 2][:, :], ps_pt[u % 2][0:S, 0:GROUPS * S], ACT.Copy).then_inc(pt_copied, 1)

                def copy_scores(units):
                    act.activation(scores[1 - par][:, units.start * GROUPS:units.stop * GROUPS, :]
                                   .rearrange("p (u g) s -> p u (g s)", g=GROUPS),
                                   ps_scores[0:S, units, 0:GROUPS * S], ACT.Copy).then_inc(
                                       upper_copied if units.start else scores_copied, 1)

                def copy_keys(first, last):
                    for g in range(first, min(last, ON_ACT)):
                        key_block(lambda o, i: act.activation(o, i, ACT.Copy), g).then_inc(k_copied, 1)

                if active(3):
                    copy_turned(0)
                if active(1):
                    act.wait_ge(scores_done, (s - 1) * 2 + 1)
                    after(act, shifted, s - 2)
                    copy_scores(slice(2, 4))
                if active(3):
                    copy_turned(1)
                if active(4):
                    b = s - 4
                    act.wait_ge(ot_done, s - 3)
                    dst = o_t[:, :, b * S:(b + 1) * S] if isinstance(b, int) else o_t[:, :, bass.ds(b * S, S)]
                    act.activation(dst, ps_ot, ACT.Copy).then_inc(ot_copied, 1)
                if active(1):
                    act.wait_ge(scores_done, s * 2)
                    copy_scores(slice(0, 2))
                if active(0) and par == 0:
                    act.wait_ge(qk_done, s + 1)
                    copy_keys(0, 1)
                if active(3):
                    copy_turned(2)
                if active(0) and par == 0:
                    copy_keys(1, 2)
                if active(3):
                    copy_turned(3)
                if active(0) and par == 0:
                    copy_keys(2, GROUPS)
                    act.wait_ge(qk_done, s + 2)
                    act.activation(q_t[:, :, :].rearrange("p (a u) s -> p a (u s)", a=2), ps_scores[:, 0:2, 0:2 * PAIR],
                                   ACT.Copy).then_inc(q_copied, 2)
                if active(2):
                    act.wait_ge(shifted, s - 1)
                    act.activation(probs[par][:, :, :], probs[par][:, :, :], ACT.Exp,
                                   scale=float(DH) ** -0.5).then_inc(exp_done, 1)
                if active(1):
                    act.wait_ge(v_done, s)
                    after(act, pv_unit, (s - 2) * UNITS)
                    act.activation(v_sb[1 - par][:, :, 0:DH], ps_v.rearrange("p (h d) -> p h d", h=HEADS),
                                   ACT.Copy).then_inc(v_copied, 1)
            run(act, body)

        @block.tensor
        def _(pe):
            def body(s, quarter, active):
                par = quarter % 2
                at = (1 - par) * S

                def score(u):
                    if u == 2:
                        pe.wait_ge(q_copied, s + par)
                        pe.wait_ge(k_copied, (s + par) * 2)
                        after(pe, scores_copied, s - 1)
                    mm = pe.matmul(ps_scores[0:S, u, 0:GROUPS * S], q_t[:, u, at:at + S], k_diag[:, u, :, at:at + S],
                                   start=True, stop=True)
                    if u in (1, 3):
                        mm.then_inc(scores_done, 1)

                def values():
                    after(pe, v_copied, s - 1)
                    pe.matmul(ps_v, c_pair[(quarter - 1) % 4 // 2][:, at:at + S], w_v[:, :], start=True, stop=True).then_inc(v_done, 1)

                def turn_output():
                    pe.wait_ge(o_ready, s - 3)
                    for k in range(DK):
                        mm = pe.transpose(ps_ot[:, k, :],
                                          o_norm[:, k * (P // DH):(k + 1) * (P // DH), :].rearrange("p h d -> p (h d)"),
                                          ident[0:S, 0:S])
                    mm.then_inc(ot_done, 1)

                def turn(u):
                    n = (s - 3) * UNITS + u
                    if u == 0:
                        pe.wait_ge(exp_done, s - 2)
                    after(pe, pt_copied, n - 1)
                    for g in range(GROUPS):
                        mm = pe.transpose(ps_pt[u % 2][0:S, g * S:(g + 1) * S], probs[1 - par][:, u * GROUPS + g, :],
                                          ident[0:S, 0:S])
                    mm.then_inc(pt_done, 1)

                def times_v(u):
                    n = (s - 3) * UNITS + u
                    if u == 0:
                        pe.wait_ge(v_copied, s - 2)
                        after(pe, o_ready, s - 3)
                        after(pe, ot_copied, s - 3)
                    pe.wait_ge(pt_copied, n + 1)
                    for g in range(GROUPS):
                        mm = pe.matmul(ps_o[:, u * GROUPS + g, :], p_t[u % 2][:, g * S:(g + 1) * S],
                                       v_sb[1 - par][:, u * GROUPS + g, :], start=True, stop=True)
                    mm.then_inc(pv_unit, 1)

                def project(n):
                    if n == 1:
                        pe.wait_ge(pair_ready, s + 2)
                        after(pe, upper_copied, s)
                    else:
                        after(pe, scores_copied, s)
                    for u in range(UNITS):
                        mm = pe.matmul(ps_scores[:, 2 * n + u // 2, (u % 2) * PAIR:(u % 2 + 1) * PAIR],
                                       w_qk[n][:, u, :], c_pair[quarter // 2][:, :], start=True, stop=True)
                    mm.then_inc(qk_done, 1)

                if active(1):
                    score(2)
                if active(3):
                    turn(0)
                if active(1):
                    score(3)
                if active(3):
                    turn(1)
                if active(4):
                    turn_output()
                if active(1):
                    score(0)
                    values()
                    score(1)
                if active(0) and par == 0:
                    project(1)
                if active(3):
                    times_v(0)
                    turn(2)
                if active(3):
                    times_v(1)
                    turn(3)
                if active(0) and par == 0:
                    project(0)
                if active(3):
                    times_v(2)
                    times_v(3)
            run(pe, body)

        @block.vector
        def _(dve):
            def body(s, quarter, active):
                par = quarter % 2
                if active(2):
                    dve.wait_ge(causal_done, s - 1)
                    dve.tensor_scalar(zeros_out[:, :, :], scores[par][:, :, :], 0.0, MASKED, ALU.is_equal,
                                      ALU.mult).then_inc(zero_marked, 1)
                if active(4):
                    dve.wait_ge(pv_unit, (s - 3) * UNITS)
                    dve.reciprocal(inv_sum[:, :], ps_o[:, :, DH]).then_inc(inv_done, 1)
                    dve.wait_ge(inv_done, s - 3)
                    after(dve, ot_done, s - 4)
                    dve.tensor_tensor(o_norm[:, :, :], ps_o[:, :, 0:DH],
                                      inv_sum[:, :].unsqueeze(2).to_broadcast([S, HEADS, DH]),
                                      ALU.mult).then_inc(o_ready, 1)
                if active(2):
                    dve.wait_ge(zero_marked, s - 1)
                    dve.tensor_tensor(scores[par][:, :, :], scores[par][:, :, :], zeros_out[:, :, :],
                                      ALU.add).then_inc(zero_masked, 1)
                    dve.wait_ge(zero_masked, s - 1)
                    dve.tensor_reduce(row_max[:, :], scores[par][:, :, :], AX.X, ALU.max).then_inc(max_done, 1)
                    dve.wait_ge(max_done, s - 1)
                    after(dve, pt_done, (s - 3) * UNITS)
                    dve.tensor_tensor(probs[par][:, :, :], scores[par][:, :, :],
                                      row_max[:, :].unsqueeze(2).to_broadcast([S, HEADS, S]),
                                      ALU.subtract).then_inc(shifted, 1)
                if active(0) and par == 0:
                    dve.wait_ge(qk_done, s + 1)
                    for g in range(ON_ACT, GROUPS):
                        key_block(dve.tensor_copy, g).then_inc(k_copied, 1)
            run(dve, body)


def output(nc, sb, ps, sem, env):
    ALU, ACT = env["ALU"], env["ACT"]
    normed_rows = env["normed_rows"]
    out, rows, scores_all, ident, minus_half, w_o_sb, gate_sb, o_t = (
        env[n] for n in ("out", "rows", "scores_all", "ident", "minus_half", "w_o_sb", "gate_sb", "o_t"))
    with ExitStack() as ctx:
        o_tile = [sb(ctx, f"o_tile{n}", [P, DK, P]) for n in range(2)]
        h_out = [sb(ctx, f"h_out{n}", [P, D]) for n in range(2)]
        stats2 = sb(ctx, "stats2", [P, 6])
        mv2 = [sb(ctx, f"mv2{n}", [P, 2]) for n in range(2)]
        rstd2 = [sb(ctx, f"rstd2{n}", [P, 1]) for n in range(2)]
        xn2 = [sb(ctx, f"xn2{n}", [P, D]) for n in range(2)]
        xn2_t = [sb(ctx, f"xn2_t{n}", [P, DK, P]) for n in range(2)]
        ps_wo = [ps(ctx, f"ps_wo{n}", [P, 512])[:, 0:D] for n in range(2)]
        ps_x2t = [ps(ctx, f"ps_x2t{n}", [P, 512])[:, 0:D].rearrange("p (k s) -> p k s", k=DK) for n in range(2)]
        ps_gate = [ps(ctx, f"ps_gate{n}", [P, 512])[:, 0:E] for n in range(2)]
        o_ready, wo_done, h_out_ready = sem("o_tile_ready"), sem("wo_done"), sem("h_out_ready")
        h_stored = [sem(f"h_stored{n}") for n in range(2)]
        stats2_done, aggr2, mv2_done, rstd2_done = (
            sem("stats2_done"), sem("aggr2"), sem("mv2_done"), sem("rstd2_done"))
        xn2_ready = sem("xn2_ready")
        xn2_stored = [sem(f"xn2_stored{n}") for n in range(2)]
        x2t_done, x2t_copied, gate_done, gate_copied = (
            sem("x2t_done"), sem("x2t_copied"), sem("gate_done"), sem("gate_copied"))
        N = TOKEN_TILES
        HEAD, ALL = 7, N + 4
        END = HEAD + (N - HEAD) // UNROLL * UNROLL
        block = ctx.enter_context(nc.Block())

        def run(eng, body):
            peeled = run_steps(eng, body, HEAD, END, N)
            for s in range(END, ALL):
                peeled(s, N)

        @block.sync
        def _(sp):
            def body(s, par, active):
                if active(1):
                    sp.wait_ge(h_out_ready, s)
                    b = s - 1
                    dst = out[b * P:(b + 1) * P, :] if isinstance(b, int) else out[bass.ds(b * P, P), :]
                    sp.dma_start(dst, h_out[1 - par][:, :]).then_inc(h_stored[1 - par], 16)
                if active(2):
                    sp.wait_ge(xn2_ready, s - 1)
                    b = s - 2
                    dst = normed_rows[b * P:(b + 1) * P, :] if isinstance(b, int) else normed_rows[bass.ds(b * P, P), :]
                    sp.dma_start(dst, xn2[par][:, :]).then_inc(xn2_stored[par], 16)
            run(sp, body)
            for n in range(2):
                sp.wait_ge(h_stored[n], 16 * len(range(n, N, 2)))
                sp.wait_ge(xn2_stored[n], 16 * len(range(n, N, 2)))

        @block.gpsimd
        def _(pool):
            def body(s, par, active):
                if active(1):
                    pool.wait_ge(mv2_done, s)
                    after(pool, xn2_ready, s - 2)
                    pool.tensor_tensor(rstd2[1 - par][:, :], mv2[1 - par][:, 1:2], minus_half[:, 0:1], ALU.pow).then_inc(rstd2_done, 1)
            run(pool, body)

        @block.scalar
        def _(act):
            def body(s, par, active):
                if active(0):
                    after(act, wo_done, s - 1)
                    src = o_t[:, :, s * P:(s + 1) * P] if isinstance(s, int) else o_t[:, :, bass.ds(s * P, P)]
                    act.activation(o_tile[par][:, :, :], src, ACT.Copy).then_inc(o_ready, 1)
                if active(3):
                    act.wait_ge(x2t_done, s - 2)
                    after(act, gate_done, s - 4)
                    act.activation(xn2_t[1 - par][:, :, :], ps_x2t[1 - par], ACT.Copy).then_inc(x2t_copied, 1)
            run(act, body)

        @block.tensor
        def _(pe):
            def body(s, par, active):
                if active(0):
                    pe.wait_ge(o_ready, s + 1)
                    after(pe, h_out_ready, s - 1)
                    for k in range(DK):
                        mm = pe.matmul(ps_wo[par], o_tile[par][:, k, :], w_o_sb[:, k, :], start=(k == 0),
                                       stop=(k == DK - 1))
                    mm.then_inc(wo_done, 1)
                if active(2):
                    pe.wait_ge(xn2_ready, s - 1)
                    after(pe, x2t_copied, s - 3)
                    for k in range(DK):
                        mm = pe.transpose(ps_x2t[par][:, k, :], xn2[par][:, k * P:(k + 1) * P], ident[:, :])
                    mm.then_inc(x2t_done, 1)
                if active(3):
                    pe.wait_ge(x2t_copied, s - 2)
                    after(pe, gate_copied, s - 4)
                    for k in range(DK):
                        mm = pe.matmul(ps_gate[1 - par], xn2_t[1 - par][:, k, :], gate_sb[:, k, :], start=(k == 0),
                                       stop=(k == DK - 1))
                    mm.then_inc(gate_done, 1)
            run(pe, body)

        @block.vector
        def _(dve):
            def body(s, par, active):
                if active(1):
                    b = s - 1
                    dve.wait_ge(wo_done, s)
                    after(dve, h_stored[1 - par], 16 * (b // 2) if isinstance(b, int) else (b - (1 - par)) * 8)
                    dve.tensor_tensor(h_out[1 - par][:, :], ps_wo[1 - par], row_of(rows, b),
                                      ALU.add).then_inc(h_out_ready, 1)
                if active(2):
                    dve.wait_ge(rstd2_done, s - 1)
                    after(dve, x2t_done, s - 3)
                    after(dve, xn2_stored[par], 16 * ((s - 2) // 2) if isinstance(s, int) else (s - 2 - par) * 8)
                    dve.tensor_scalar(xn2[par][:, :], h_out[par][:, :], mv2[par][:, 0:1], rstd2[par][:, 0:1], ALU.subtract,
                                      ALU.mult).then_inc(xn2_ready, 1)
                if active(1):
                    dve.wait_ge(h_out_ready, s)
                    dve.bn_stats(stats2[:, :], h_out[1 - par][:, :]).then_inc(stats2_done, 1)
                    dve.wait_ge(stats2_done, s)
                if active(4):
                    b = s - 4
                    dve.wait_ge(gate_done, b + 1)
                    dst = (scores_all[:, b, :] if isinstance(b, int)
                           else scores_all[:, bass.ds(b, 1), :].rearrange("p a e -> p (a e)"))
                    dve.tensor_copy(dst, ps_gate[par]).then_inc(gate_copied, 1)
                if active(1):
                    dve.bn_aggr(mv2[1 - par][:, :], stats2[:, :]).then_inc(aggr2, 1)
                    dve.wait_ge(aggr2, s)
                    dve.tensor_scalar(mv2[1 - par][:, 1:2], mv2[1 - par][:, 1:2], EPS, None, ALU.add).then_inc(mv2_done, 1)
            run(dve, body)


def route_and_experts(nc, outer, sb, ps, sem, env):
    fp32, i32, ALU, ACT, AX = env["fp32"], env["i32"], env["ALU"], env["ACT"], env["AX"]
    out, normed_rows, scores_all, ident = (env[n] for n in ("out", "normed_rows", "scores_all", "ident"))

    NT = TOKEN_TILES
    ctx = ExitStack()
    with ctx:
        W12 = [*env["W12"], sb(ctx, "W12_1", [P, E * 2 * HID])]
        tie_rank = sb(ctx, "tie_rank", [P, E])
        before = sb(ctx, "before", [P, P])
        ones = sb(ctx, "ones", [P, P])
        iota_i = sb(ctx, "iota_i", [P, P], i32)
        token_i = sb(ctx, "token_i", [P, NT], i32)
        first = [sb(ctx, f"first{n}", [P, NT, E]) for n in range(TOP)]
        work = sb(ctx, "work", [P, NT, E])
        work2 = sb(ctx, "work2", [P, NT, E])
        rest = sb(ctx, "rest", [P, NT, E])
        top = [sb(ctx, f"top{n}", [P, NT]) for n in range(TOP)]
        small = sb(ctx, "small", [P, NT])
        both = sb(ctx, "both", [P, NT, E])
        running = sb(ctx, "running", [P, NT, E])
        count_i = sb(ctx, "count_i", [P, E], i32)
        tiles_f = sb(ctx, "tiles_f", [P, E])
        tile_end = sb(ctx, "tile_end", [P, E])
        tile_start = sb(ctx, "tile_start", [P, E])
        slot_f = sb(ctx, "slot_f", [P, TOP, NT])
        slot_i = sb(ctx, "slot_i", [P, TOP, NT], i32)
        tile_no = sb(ctx, "tile_no", [P, TILES])
        token_f = sb(ctx, "token_f", [P, NT])
        prob = sb(ctx, "prob", [P, TOP, NT])
        slot_tile_i = sb(ctx, "slot_tile_i", [P, TOP, NT], i32)
        slot_tile = sb(ctx, "slot_tile", [P, TOP, NT])
        slot_row = sb(ctx, "slot_row", [P, TOP, NT])
        place_i = sb(ctx, "place_i", [P, P], i32)
        place = sb(ctx, "place", [P, P])
        at_row = [sb(ctx, f"at_row{n}", [P, P]) for n in range(4)]
        at_tile = [sb(ctx, f"at_tile{n}", [P, 2, TILES]) for n in range(4)]
        owner = sb(ctx, "owner", [P, TILES])
        owner_p = sb(ctx, "owner_p", [P, TILES])
        source_i = sb(ctx, "source_i", [P, TILES], i32)
        target_i = sb(ctx, "target_i", [P, TILES], i32)
        tile_expert = sb(ctx, "tile_expert", [1, TILES])
        tile_expert_i = sb(ctx, "tile_expert_i", [1, TILES], i32)
        trash_row = sb(ctx, "trash_row", [P, 1])

        x_in = [sb(ctx, f"x_in{n}", [P, D]) for n in range(2)]
        source = [sb(ctx, f"source{n}", [P, 1], i32) for n in range(2)]
        x_t = [sb(ctx, f"x_t{n}", [P, DK, P]) for n in range(2)]
        gated = sb(ctx, "gated", [P, HID])
        hidden = [sb(ctx, f"hidden{n}", [P, HID]) for n in range(2)]
        hidden_t = [sb(ctx, f"hidden_t{n}", [P, HK, P]) for n in range(1)]
        y_sb = [sb(ctx, f"y_sb{n}", [P, D]) for n in range(2)]
        weight = [sb(ctx, f"weight{n}", [P, 1]) for n in range(2)]
        pad_row = sb(ctx, "pad_row", [P, TILES])
        dest = [sb(ctx, f"dest{n}", [P, 1], i32) for n in range(2)]

        ps_xt = ps(ctx, "ps_xt_moe", [P, DK, P])
        ps_h = [ps(ctx, f"ps_h{n}", [P, 2, HID]) for n in range(2)]
        ps_ht = ps(ctx, "ps_ht", [P, HK, P])
        ps_y = ps(ctx, "ps_y", [P, 512])
        ps_prefix = ps_h[0][:, 0, 0:TOKEN_TILES * E]
        ps_owner = ps_h[1][:, 0, 0:2 * TILES]
        ps_total = ps_h[0][:, 1, 0:TOKEN_TILES * E]

        W3 = env["W3"]
        weights_in = sem("weights_in")
        made = sem("route_consts")
        chain = sem("route_chain")
        both_ready, prefix_done = sem("both_ready"), sem("prefix_done")
        gap_ready, gap_exp = sem("gap_ready"), sem("gap_exp")
        slots_ready, tile_expert_ready = sem("slots_ready"), sem("tile_expert_ready")
        x_loaded = [sem(f"x_loaded{n}") for n in range(2)]
        xt_done, xt_copied = sem("moe_xt_done"), sem("moe_xt_copied")
        h_done, silu_done, hidden_ready = sem("h_done"), sem("silu_done"), sem("hidden_ready")
        ht_done, ht_copied = sem("ht_done"), sem("ht_copied")
        y_done, y_ready = sem("y_done"), sem("y_ready")
        source_known, weight_known, dest_known = sem("source_known"), sem("weight_known"), sem("dest_known")
        row_marked, tile_marked, prob_marked = sem("row_marked"), sem("tile_marked"), sem("prob_marked")
        slots_split, entry_added = sem("slots_split"), sem("entry_added")
        y_added = sem("y_added")

        AHEAD = 2
        HEAD, END, ALL = 8, TILES - 4, TILES + 2
        ENTRIES = [(t, n) for t in range(NT) for n in range(TOP)]

        def by_pool(i):
            return i % 4 != 0

        block = ctx.enter_context(nc.Block())

        @block.gpsimd
        def _(pool):
            pool.iota(token_i[:, :], pattern=[[P, NT]], base=1, channel_multiplier=1).then_inc(made, 1)
            pool.iota(iota_i[:, 0:E], pattern=[[-1, E]], base=E, channel_multiplier=0).then_inc(made, 1)
            pool.iota(iota_i[:, E:E + TILES], pattern=[[1, TILES]], base=0, channel_multiplier=0).then_inc(made, 1)
            pool.iota(iota_i[:, P - 1:P], pattern=[[0, 1]], base=0, channel_multiplier=1).then_inc(made, 1)
            pool.iota(place_i[:, :], pattern=[[1, P]], base=0, channel_multiplier=0).then_inc(made, 1)
            pool.memset(ones[:, :], 1.0).then_inc(made, 1)
            pool.wait_ge(made, 6)
            pool.affine_select(out=before[:, :], in_=ones[:, :], compare_op=ALU.is_gt, fill=0.0, base=0,
                               pattern=[[1, P]], channel_multiplier=-1).then_inc(made, 1)
            pool.wait_ge(slots_split, 1)
            for i, (b, n) in enumerate(ENTRIES):
                if by_pool(i):
                    after(pool, entry_added, i - 3)
                    pool.tensor_scalar(at_tile[i % 4][:, 1, :], tile_no[:, :], slot_tile[:, n, b:b + 1],
                                       prob[:, n, b:b + 1], ALU.is_equal, ALU.mult).then_inc(prob_marked, 1)

            last_row = pool.to_reg(OUT_ROWS - 1)
            last_token = pool.to_reg(PADDED - 1)

            def gather(par):
                pool.indirect_dma_start(
                    out=x_in[par][:, :], out_offset=None, in_=normed_rows[:, :],
                    in_offset=bass.IndirectOffsetOnAxis(ap=source[par][:, 0:1], axis=0),
                    bounds_check=last_token).then_inc(x_loaded[par], 16)

            for n in range(AHEAD):
                pool.wait_ge(source_known, n + 1)
                gather(n)

            def body(s, par, active):
                if active(-AHEAD):
                    known = s + AHEAD + 1 if isinstance(s, int) else pool.to_reg(s + AHEAD + 1)
                    turned = s + 1 if isinstance(s, int) else pool.to_reg(s + 1)
                    pool.wait_ge(slots_ready, 1)
                    pool.wait_ge(source_known, known)
                    pool.wait_ge(xt_done, turned)
                    gather(par)
                if active(2):
                    t = s - 2
                    added = 16 * t if isinstance(t, int) else pool.to_reg(t * 16)
                    done = t + 1 if isinstance(t, int) else pool.to_reg(t + 1)
                    pool.wait_ge(slots_ready, 1)
                    after(pool, y_added, added)
                    pool.wait_ge(y_ready, done)
                    pool.wait_ge(dest_known, done)
                    pool.indirect_dma_start(
                        out=out[:, :], out_offset=bass.IndirectOffsetOnAxis(ap=dest[par][:, 0:1], axis=0),
                        in_=y_sb[par][:, :], in_offset=None, bounds_check=last_row,
                        compute_op=ALU.add).then_inc(y_added, 16)

            peeled = run_steps(pool, body, HEAD, END, TILES)
            for s in range(END, ALL):
                peeled(s, TILES)
            pool.wait_ge(y_added, 16 * TILES)

        @block.vector
        def _(dve):
            links = [0]

            def link(ins):
                links[0] += 1
                ins.then_inc(chain, 1)
                dve.wait_ge(chain, links[0])

            def per_expert(ap):
                return ap.unsqueeze(2).to_broadcast([P, NT, E])

            dve.wait_ge(made, 7)
            link(dve.tensor_copy(tie_rank[:, :], iota_i[:, 0:E]))
            link(dve.tensor_copy(tile_no[:, :], iota_i[:, E:E + TILES]))
            link(dve.tensor_copy(place[:, :], place_i[:, :]))
            link(dve.tensor_copy(token_f[:, :], token_i[:, :]))
            link(dve.tensor_scalar(trash_row[:, :], iota_i[:, P - 1:P], float(TOKENS + 1), None, ALU.add))

            ranks = tie_rank[:, :].unsqueeze(1).to_broadcast([P, NT, E])
            scores = scores_all
            for n in range(TOP):
                link(dve.tensor_reduce(top[n][:, :], scores[:, :, :], AX.X, ALU.max))
                link(dve.tensor_tensor(work[:, :, :], scores[:, :, :], per_expert(top[n][:, :]), ALU.is_equal))
                link(dve.tensor_tensor(work[:, :, :], work[:, :, :], ranks, ALU.mult))
                link(dve.tensor_reduce(small[:, :], work[:, :, :], AX.X, ALU.max))
                link(dve.tensor_tensor(first[n][:, :, :], work[:, :, :], per_expert(small[:, :]), ALU.is_equal))
                if n == 0:
                    link(dve.scalar_tensor_tensor(rest[:, :, :], first[0][:, :, :], MASKED, scores_all[:, :, :],
                                                  ALU.mult, ALU.add))
                    scores = rest
            link(dve.tensor_tensor(both[:, :, :], first[0][:, :, :], first[1][:, :, :], ALU.add))
            dve.memset(both[TOKENS - (NT - 1) * P:P, NT - 1, :], 0.0).then_inc(both_ready, 1)
            dve.tensor_tensor(small[:, :], top[1][:, :], top[0][:, :], ALU.subtract).then_inc(gap_ready, 1)
            dve.wait_ge(gap_exp, 1)
            link(dve.tensor_scalar(top[0][:, :], small[:, :], 1.0, None, ALU.add))
            link(dve.reciprocal(top[1][:, :], top[0][:, :]))
            link(dve.tensor_copy(prob[:, 0, :], top[1][:, :]))
            link(dve.tensor_tensor(prob[:, 1, :], top[1][:, :], small[:, :], ALU.mult))

            dve.wait_ge(prefix_done, 1)
            link(dve.tensor_copy(work[:, :, :], ps_total.rearrange("p (b e) -> p b e", e=E)))
            for e in range(E):
                last = dve.tensor_tensor_scan(running[:, :, e], ones[:, 0:NT], work[:, :, e], 0.0, ALU.mult, ALU.add)
            link(last)
            link(dve.tensor_scalar(count_i[:, :], running[:, NT - 1, :], float(P - 1), None, ALU.add))
            link(dve.tensor_scalar(count_i[:, :], count_i[:, :], P.bit_length() - 1, None, ALU.arith_shift_right))
            link(dve.tensor_copy(tiles_f[:, :], count_i[:, :]))
            link(dve.tensor_tensor_scan(tile_end[:, :], ones[:, 0:E], tiles_f[:, :], 0.0, ALU.mult, ALU.add))
            link(dve.tensor_tensor(tile_start[:, :], tile_end[:, :], tiles_f[:, :], ALU.subtract))
            link(dve.tensor_scalar(tiles_f[:, :], tile_start[:, :], float(P), None, ALU.mult))
            link(dve.tensor_tensor(work2[:, :, :], running[:, :, :], work[:, :, :], ALU.subtract))
            link(dve.tensor_tensor(work2[:, :, :], work2[:, :, :], ps_prefix.rearrange("p (b e) -> p b e", e=E), ALU.add))
            link(dve.tensor_tensor(work2[:, :, :], work2[:, :, :],
                                   tiles_f[:, :].unsqueeze(1).to_broadcast([P, NT, E]), ALU.add))
            for n in range(TOP):
                link(dve.tensor_tensor(work[:, :, :], work2[:, :, :], first[n][:, :, :], ALU.mult))
                link(dve.tensor_reduce(slot_f[:, n, :], work[:, :, :], AX.X, ALU.add))
            link(dve.tensor_copy(slot_i[:, :, :], slot_f[:, :, :]))
            link(dve.tensor_scalar(slot_tile_i[:, :, :], slot_i[:, :, :], P.bit_length() - 1, None,
                                   ALU.arith_shift_right))
            link(dve.tensor_copy(slot_tile[:, :, :], slot_tile_i[:, :, :]))
            dve.scalar_tensor_tensor(slot_row[:, :, :], slot_tile[:, :, :], -float(P), slot_f[:, :, :],
                                     ALU.mult, ALU.add).then_inc(slots_split, 1)
            dve.wait_ge(slots_split, 1)
            for i, (b, n) in enumerate(ENTRIES):
                after(dve, entry_added, i - 3)
                dve.tensor_scalar(at_row[i % 4][:, :], place[:, :], slot_row[:, n, b:b + 1], None,
                                  ALU.is_equal).then_inc(row_marked, 1)
                if not by_pool(i):
                    dve.tensor_scalar(at_tile[i % 4][:, 1, :], tile_no[:, :], slot_tile[:, n, b:b + 1],
                                      prob[:, n, b:b + 1], ALU.is_equal, ALU.mult)
                dve.tensor_scalar(at_tile[i % 4][:, 0, :], tile_no[:, :], slot_tile[:, n, b:b + 1], token_f[:, b:b + 1],
                                  ALU.is_equal, ALU.mult).then_inc(tile_marked, 1)
            link(dve.tensor_scalar(tile_expert[:, :], tile_no[0:1, :], tile_start[0:1, 1:2], None, ALU.is_ge))
            for e in range(2, E):
                link(dve.scalar_tensor_tensor(tile_expert[:, :], tile_no[0:1, :], tile_start[0:1, e:e + 1],
                                              tile_expert[:, :], ALU.is_ge, ALU.add))
            dve.tensor_copy(tile_expert_i[:, :], tile_expert[:, :]).then_inc(tile_expert_ready, 1)

            dve.wait_ge(entry_added, len(ENTRIES))
            link(dve.tensor_copy(owner[:, :], ps_owner[:, 0:TILES]))
            link(dve.tensor_copy(owner_p[:, :], ps_owner[:, TILES:2 * TILES]))
            link(dve.tensor_scalar(source_i[:, :], owner[:, :], -1.0, 0.0, ALU.add, ALU.max))
            link(dve.tensor_scalar(pad_row[:, :], owner[:, :], 0.0, trash_row[:, 0:1], ALU.is_equal, ALU.mult))
            dve.scalar_tensor_tensor(target_i[:, :], pad_row[:, :], -1.0, owner[:, :], ALU.add,
                                     ALU.add).then_inc(slots_ready, 1)
            dve.wait_ge(slots_ready, 1)

            def column(table, t):
                return table[:, t:t + 1] if isinstance(t, int) else table[:, bass.ds(t, 1)]

            for n in range(AHEAD):
                dve.tensor_copy(source[n][:, :], column(source_i, n)).then_inc(source_known, 1)

            def body(s, par, active):
                if active(-AHEAD):
                    dve.wait_ge(x_loaded[par], parity_count(1, s, par))
                    dve.tensor_copy(source[par][:, :], column(source_i, s + AHEAD)).then_inc(source_known, 1)
                if active(1):
                    t = s - 1
                    dve.wait_ge(silu_done, t + 1)
                    after(dve, ht_done, t - 1)
                    dve.tensor_tensor(hidden[1 - par][:, :], gated[:, :], ps_h[1 - par][:, 1, :],
                                      ALU.mult).then_inc(hidden_ready, 1)
                if active(2):
                    t = s - 2
                    after(dve, y_added, 16 * (t - 1) if isinstance(t, int) else (t - 1) * 16)
                    dve.tensor_copy(dest[par][:, :], column(target_i, t)).then_inc(dest_known, 1)
                    dve.tensor_copy(weight[par][:, :], column(owner_p, t)).then_inc(weight_known, 1)
                    dve.wait_ge(y_done, t + 1)
                    dve.wait_ge(weight_known, t + 1)
                    after(dve, y_added, 16 * (t - 1) if isinstance(t, int) else (t - 1) * 16)
                    dve.tensor_scalar(y_sb[par][:, :], ps_y[:, 0:D], weight[par][:, 0:1], None,
                                      ALU.mult).then_inc(y_ready, 1)

            peeled = run_steps(dve, body, HEAD, END, TILES)
            for s in range(END, ALL):
                peeled(s, TILES)

        @block.scalar
        def _(act):
            for k in range(1, DK):
                for e in range(E):
                    act.dma_start(W12[k][:, e * 2 * HID:(e + 1) * 2 * HID],
                                  env["w12"][e, k * P:(k + 1) * P, :]).then_inc(weights_in, 16)
            act.wait_ge(gap_ready, 1)
            act.activation(small[:, :], small[:, :], ACT.Exp).then_inc(gap_exp, 1)

            def body(s, par, active):
                if active(0):
                    act.wait_ge(xt_done, s + 1)
                    after(act, h_done, s - 1)
                    act.activation(x_t[par][:, :, :], ps_xt[:, :, :], ACT.Copy).then_inc(xt_copied, 1)
                if active(2):
                    act.wait_ge(ht_done, s - 1)
                    act.activation(hidden_t[0][:, :, :], ps_ht[:, :, :], ACT.Copy).then_inc(ht_copied, 1)
                if active(1):
                    act.wait_ge(h_done, s)
                    after(act, hidden_ready, s - 1)
                    act.activation(gated[:, :], ps_h[1 - par][:, 0, :], ACT.Silu).then_inc(silu_done, 1)

            peeled = run_steps(act, body, HEAD, END, TILES)
            for s in range(END, ALL):
                peeled(s, TILES)

        @block.tensor
        def _(pe):
            pe.wait_ge(both_ready, 1)
            pe.wait_ge(made, 7)
            choice = both[:, :, :].rearrange("p b e -> p (b e)")
            pe.matmul(ps_prefix, before[:, :], choice, start=True, stop=True)
            pe.matmul(ps_total, ones[:, :], choice, start=True, stop=True).then_inc(prefix_done, 1)
            for i, (b, n) in enumerate(ENTRIES):
                real = min(P, TOKENS - b * P)
                pe.wait_ge(row_marked, i + 1)
                pe.wait_ge(tile_marked, i + 1)
                after(pe, prob_marked, sum(by_pool(j) for j in range(i + 1)))
                pe.matmul(ps_owner, at_row[i % 4][0:real, :],
                          at_tile[i % 4][0:real, :, :].rearrange("p a t -> p (a t)"),
                          start=(i == 0), stop=(i == len(ENTRIES) - 1)).then_inc(entry_added, 1)
            pe.wait_ge(slots_ready, 1)
            pe.wait_ge(tile_expert_ready, 1)
            pe.wait_ge(weights_in, 16 * E)

            def body(s, par, active):
                if active(1):
                    up_expert = expert_of(s - 1)
                if active(2):
                    down_expert = expert_of(s - 2)
                if active(0):
                    pe.wait_ge(x_loaded[par], 16 * (s // 2 + 1) if isinstance(s, int) else (s - par + 2) * 8)
                    after(pe, xt_copied, s)
                    for k in range(DK):
                        mm = pe.transpose(ps_xt[:, k, :], x_in[par][:, k * P:(k + 1) * P], ident[:, :])
                    mm.then_inc(xt_done, 1)
                if active(2):
                    pe.wait_ge(hidden_ready, s - 1)
                    for c in range(HK):
                        mm = pe.transpose(ps_ht[:, c, :], hidden[par][:, c * P:(c + 1) * P], ident[:, :])
                    mm.then_inc(ht_done, 1)
                if active(1):
                    t = s - 1
                    pe.wait_ge(xt_copied, t + 1)
                    after(pe, hidden_ready, t - 1)
                    for half in range(2):
                        for k in range(DK):
                            mm = pe.matmul(ps_h[1 - par][:, half, :], x_t[1 - par][:, k, :],
                                           W12[k][:, bass.ds(up_expert * (2 * HID) + half * HID, HID)],
                                           start=(k == 0), stop=(k == DK - 1))
                    mm.then_inc(h_done, 1)
                if active(2):
                    t = s - 2
                    pe.wait_ge(ht_copied, t + 1)
                    after(pe, y_ready, t)
                    for c in range(HK):
                        mm = pe.matmul(ps_y[:, 0:D], hidden_t[0][:, c, :],
                                       W3[:, bass.ds(down_expert * (HK * D) + c * D, D)],
                                       start=(c == 0), stop=(c == HK - 1))
                    mm.then_inc(y_done, 1)

            def expert_of(t):
                at = tile_expert_i[0:1, t:t + 1] if isinstance(t, int) else tile_expert_i[0:1, bass.ds(t, 1)]
                return pe.value_load(at, min_val=0, max_val=E - 1)

            peeled = run_steps(pe, body, HEAD, END, TILES)
            for s in range(END, ALL):
                peeled(s, TILES)


def kernel(**inputs):
    import numpy as np
    import concourse.bacc as bacc
    from concourse import mybir as mb
    from concourse.bass_utils import run_bass_kernel_spmd

    a = {k: np.asarray(v) for k, v in inputs.items()}
    side = 16
    grid = 6
    x = a["x"].reshape(BATCH, 3, grid, side, grid, side)
    patches = x.transpose(1, 3, 5, 0, 2, 4).reshape(F, IMG_TOKENS)

    def tile_of(block):
        return block.reshape(FK, P, -1).transpose(1, 0, 2).reshape(P, -1)

    arrays = {
        "patches": np.concatenate([tile_of(patches[:, at:at + EMB]) for at in range(0, IMG_TOKENS, EMB)], axis=1),
        "txt": a["txt"].reshape(BATCH * TXT, D),
        "w_lin": a["L0_tok_W_lin"].T,
        "b_lin": a["L0_tok_b_lin"].reshape(1, D),
        "cls": a["L0_tok_class_token"].reshape(1, D),
        "pos": a["L0_tok_position_embeddings"].reshape(1 + IMG, D),
        "w_down": np.concatenate([a["L0_attn_W_dq"], a["L0_attn_W_dkv"]], axis=1),
        "gamma": np.concatenate([a["L0_attn_q_ln_g"], a["L0_attn_kv_ln_g"]]).reshape(P, 1),
        "beta": np.concatenate([a["L0_attn_q_ln_b"], a["L0_attn_kv_ln_b"]]).reshape(P, 1),
        "w_uq": a["L0_attn_W_uq"],
        "w_ukv": a["L0_attn_W_ukv"],
        "w_o": a["L0_attn_W_o"].T,
        "w12": a["L0_ffn_w12"].transpose(0, 2, 1),
        "w3": a["L0_ffn_w3"].transpose(0, 2, 1),
        "gate": a["L0_ffn_gate_w"].T,
    }
    arrays = {k: np.ascontiguousarray(v) for k, v in arrays.items()}
    nc = bacc.Bacc("TRN2", target_bir_lowering=False, num_devices=1)
    args = {k: nc.dram_tensor(k, v.shape, mb.dt.from_np(v.dtype), kind="ExternalInput").ap() for k, v in arrays.items()}
    out = nc.dram_tensor("out", [OUT_ROWS, D], mb.dt.float32, kind="ExternalOutput").ap()
    build(nc, out=out, **args)
    r = run_bass_kernel_spmd(nc, [arrays], core_ids=[0])
    return r.results[0]["out"][0:TOKENS].reshape(BATCH, S, D)
```
